# Optimizing a Trainium2 kernel written in Bass

```python
import numpy as np
import jax
import jax.numpy as jnp

def _softmax(x, axis=-1):
    return jax.nn.softmax(x, axis=axis)

def _gelu(x):
    return jax.nn.gelu(x, approximate=True)

def _silu(x):
    return jax.nn.silu(x)

def _sigmoid(x):
    return jax.nn.sigmoid(x)

def _layernorm(x, axis=-1, eps=1e-05):
    m = jnp.mean(x, axis=axis, keepdims=True)
    v = jnp.var(x, axis=axis, keepdims=True)
    return (x - m) / jnp.sqrt(v + eps)

def _scatter_add(tgt, idx, src, axis=0):
    return tgt.at[idx].add(src)

def _segment_sum(src, seg, n):
    return jax.ops.segment_sum(src, seg, n)
kernel_name = 'mk_sandwich_d1_jaxref_r8_39612c'

def setup_inputs(seed: int=0):
    np.random.seed(seed)
    _w = jnp.asarray

    def _L0_attn_setup():
        import jax, jax.numpy as jnp
        import numpy as np
        from math import sqrt
        EMBED = 128
        HEADS = 16
        key = jax.random.key(seed)
        k1, k2, k3, k4, k5 = jax.random.split(key, 5)
        x = jax.random.normal(k1, (2, 256, EMBED), dtype=jnp.float32)
        s = 1.0 / sqrt(EMBED)
        W_qkv = jax.random.normal(k2, (EMBED, 3 * EMBED), dtype=jnp.float32) * s
        b_qkv = jax.random.normal(k3, (3 * EMBED,), dtype=jnp.float32) * 0.01
        W_out = jax.random.normal(k4, (EMBED, EMBED), dtype=jnp.float32) * s
        b_out = jax.random.normal(k5, (EMBED,), dtype=jnp.float32) * 0.01
        return {'x': x, 'W_qkv': W_qkv, 'b_qkv': b_qkv, 'W_out': W_out, 'b_out': b_out}
    _L0_attn_in = _L0_attn_setup()

    def _L0_ffn_setup():
        import jax, jax.numpy as jnp
        import numpy as np
        D_MODEL = 128
        EXPANSION = 4
        D_HIDDEN = D_MODEL * EXPANSION
        NUM_STAGES = int(np.log2(D_HIDDEN))

        def butterfly(y, weights, dim):
            lead = y.shape[:-1]
            for stage in range(weights.shape[0]):
                s = 2 ** stage
                nb = dim // (2 * s)
                yr = y.reshape(*lead, nb, 2, s)
                a = yr[..., 0, :]
                b = yr[..., 1, :]
                w = weights[stage].reshape(nb, s, 2, 2)
                na = w[..., 0, 0] * a + w[..., 0, 1] * b
                nb2 = w[..., 1, 0] * a + w[..., 1, 1] * b
                y = jnp.stack([na, nb2], axis=-2).reshape(*lead, dim)
            return y
        key = jax.random.key(seed)
        ks = jax.random.split(key, 6)
        B, S = (4, 256)
        x = jax.random.normal(ks[0], (B, S, D_MODEL), jnp.float32)
        W_exp = jax.random.normal(ks[1], (D_MODEL, D_HIDDEN), jnp.float32) * 0.02
        b_exp = jnp.zeros((D_HIDDEN,), jnp.float32)
        up_weights = jax.random.normal(ks[2], (NUM_STAGES, D_HIDDEN // 2, 2, 2), jnp.float32) * 0.02
        up_bias = jnp.zeros((D_HIDDEN,), jnp.float32)
        down_weights = jax.random.normal(ks[3], (NUM_STAGES, D_HIDDEN // 2, 2, 2), jnp.float32) * 0.02
        W_con = jax.random.normal(ks[4], (D_HIDDEN, D_MODEL), jnp.float32) * 0.02
        b_con = jnp.zeros((D_MODEL,), jnp.float32)
        down_bias = jnp.zeros((D_MODEL,), jnp.float32)
        return dict(x=x, W_exp=W_exp, b_exp=b_exp, up_weights=up_weights, up_bias=up_bias, down_weights=down_weights, W_con=W_con, b_con=b_con, down_bias=down_bias)
    _L0_ffn_in = _L0_ffn_setup()
    _d = {'L0_attn_x': _L0_attn_in['x'], 'L0_attn_W_qkv': _L0_attn_in['W_qkv'], 'L0_attn_b_qkv': _L0_attn_in['b_qkv'], 'L0_attn_W_out': _L0_attn_in['W_out'], 'L0_attn_b_out': _L0_attn_in['b_out'], 'L0_ffn_W_exp': _L0_ffn_in['W_exp'], 'L0_ffn_b_exp': _L0_ffn_in['b_exp'], 'L0_ffn_up_weights': _L0_ffn_in['up_weights'], 'L0_ffn_up_bias': _L0_ffn_in['up_bias'], 'L0_ffn_down_weights': _L0_ffn_in['down_weights'], 'L0_ffn_W_con': _L0_ffn_in['W_con'], 'L0_ffn_b_con': _L0_ffn_in['b_con'], 'L0_ffn_down_bias': _L0_ffn_in['down_bias']}
    _x0 = _d['L0_attn_x']
    _d['L0_attn_x'] = jax.random.normal(jax.random.fold_in(jax.random.key(seed), 1), (4, 1024, 128), dtype=_x0.dtype)
    del _x0
    return _d

def reference(L0_attn_x, L0_attn_W_qkv, L0_attn_b_qkv, L0_attn_W_out, L0_attn_b_out, L0_ffn_W_exp, L0_ffn_b_exp, L0_ffn_up_weights, L0_ffn_up_bias, L0_ffn_down_weights, L0_ffn_W_con, L0_ffn_b_con, L0_ffn_down_bias):

    def _L0_attn_ref(x, W_qkv, b_qkv, W_out, b_out):
        import jax, jax.numpy as jnp
        import numpy as np
        from math import sqrt
        EMBED = 128
        HEADS = 16
        B, N, E = x.shape
        H = HEADS
        d = E // H
        qkv = x @ W_qkv + b_qkv
        q, k, v = jnp.split(qkv, 3, axis=2)
        q = q.reshape(B, N, H, d)
        k = k.reshape(B, N, H, d)
        v = v.reshape(B, N, H, d)
        energy = jnp.einsum('bqhe,bkhe->bqhk', q, k)
        attn = jax.nn.softmax(energy, axis=-1) / sqrt(E)
        out = jnp.einsum('bihv,bvhd->bihd', attn, v)
        out = out.reshape(B, N, E)
        return out @ W_out + b_out

    def _L0_ffn_ref(x, W_exp, b_exp, up_weights, up_bias, down_weights, W_con, b_con, down_bias):
        import jax, jax.numpy as jnp
        import numpy as np
        D_MODEL = 128
        EXPANSION = 4
        D_HIDDEN = D_MODEL * EXPANSION
        NUM_STAGES = int(np.log2(D_HIDDEN))

        def butterfly(y, weights, dim):
            lead = y.shape[:-1]
            for stage in range(weights.shape[0]):
                s = 2 ** stage
                nb = dim // (2 * s)
                yr = y.reshape(*lead, nb, 2, s)
                a = yr[..., 0, :]
                b = yr[..., 1, :]
                w = weights[stage].reshape(nb, s, 2, 2)
                na = w[..., 0, 0] * a + w[..., 0, 1] * b
                nb2 = w[..., 1, 0] * a + w[..., 1, 1] * b
                y = jnp.stack([na, nb2], axis=-2).reshape(*lead, dim)
            return y
        h = jnp.einsum('bsd,dh->bsh', x, W_exp) + b_exp
        h = butterfly(h, up_weights, D_HIDDEN)
        h = jax.nn.gelu(h + up_bias, approximate=False)
        h = butterfly(h, down_weights, D_HIDDEN)
        y = jnp.einsum('bsh,hd->bsd', h, W_con) + b_con
        return y + down_bias
    x = L0_attn_x
    x = x + _layernorm(_L0_attn_ref(_layernorm(x, axis=-1), L0_attn_W_qkv, L0_attn_b_qkv, L0_attn_W_out, L0_attn_b_out), axis=-1)
    x = x + _layernorm(_L0_ffn_ref(_layernorm(x, axis=-1), L0_ffn_W_exp, L0_ffn_b_exp, L0_ffn_up_weights, L0_ffn_up_bias, L0_ffn_down_weights, L0_ffn_W_con, L0_ffn_b_con, L0_ffn_down_bias), axis=-1)
    return x

_drawn_inputs = setup_inputs


def setup_inputs(seed=0):
    import zlib

    import numpy as np

    out = dict(_drawn_inputs(seed))
    spreads = {'L0_ffn_b_exp': (0.0, 0.1),
     'L0_ffn_up_bias': (0.0, 0.1),
     'L0_ffn_b_con': (0.0, 0.1),
     'L0_ffn_down_bias': (0.0, 0.1)}
    factors = {'L0_attn_b_qkv': 2.925}
    for name, (base, spread) in spreads.items():
        noise = np.random.default_rng([zlib.crc32(name.encode()), seed]).standard_normal(out[name].shape)
        drawn = base * np.exp(spread * noise) if base else spread * noise
        out[name] = jnp.asarray(drawn.astype(out[name].dtype))
    for name, factor in factors.items():
        out[name] = (out[name] * factor).astype(out[name].dtype)
    return out
```

```python
import math
from contextlib import ExitStack

import numpy as np

import concourse.bass as bass
from concourse import mybir

FP32 = mybir.dt.float32
BF16 = mybir.dt.bfloat16
ALU = mybir.AluOpType
ACT = mybir.ActivationFunctionType
AX = mybir.AxisListType

P = 128
B, N, E = 4, 1024, 128
H = 16
D = E // H
HG = 4
NG = H // HG
GROUPS = B * NG
KT = N // P
TILES = B * KT
QH = N // 2
QT = QH // P
UNITS = GROUPS * 2
PARTS = 3
PROD = PARTS * PARTS * D
ROWS = PROD + PARTS
VW = D + 1
HID = 512
HC = HID // P
STAGES = int(math.log2(HID))
EPS = 1e-5
MW = 96
LEAD = 12
STEPS = KT
TB = 512
BT = TB // P
BLOCKS = B * N // TB


def attention_ffn_kernel(nc, x, w_qkv, b_qkv, w_out, b_out, w_exp, b_exp, up_w, up_b, down_w,
                         w_con, b_con, down_b, out):
    q_dram = nc.dram_tensor("q_parts", (GROUPS, PARTS, D * HG, N), BF16, kind="Internal").ap()
    k_dram = nc.dram_tensor("k_parts", (GROUPS, PARTS, D * HG, N), BF16, kind="Internal").ap()
    v_dram = nc.dram_tensor("v_ones", (GROUPS, P, KT * HG * VW), FP32, kind="Internal").ap()
    o_dram = nc.dram_tensor("o_sums", (GROUPS, 2, HG * VW, QH), FP32, kind="Internal").ap()

    ctx = ExitStack()
    with ctx:
        def sb(name, shape, dt=FP32):
            return ctx.enter_context(nc.sbuf_tensor(name, shape, dt))

        def sem(name):
            return ctx.enter_context(nc.semaphore(name))

        wqkv = sb("wqkv", [P, 3 * E])
        wqk = sb("wqk", [P, 2, E])
        brow = sb("brow", [1, 3 * E])
        brow_qk = sb("brow_qk", [1, 2, E])
        bqk = sb("bqk", [P, 2])
        bv = sb("bv", [P, E])
        wout = sb("wout", [P, E])
        bout = sb("bout", [P, E])
        wexp = sb("wexp", [P, HID])
        wcon = sb("wcon", [P, HC, E])
        bexp = sb("bexp", [1, HID])
        upb = sb("upb", [1, HID])
        bcon = sb("bcon", [P, E])
        bdown = sb("bdown", [P, E])
        bffn = sb("bffn", [P, E])
        ident = sb("ident", [P, P])
        ident_bf = sb("ident_bf", [P, P], BF16)
        one = sb("one", [1, 1])
        neghalf = sb("neghalf", [P, KT])
        eps_c = sb("eps_c", [P, KT])
        carrier = sb("carrier", [P, 1])

        wst = sb("wst", [P, 2, 4 * HID // 2])
        up_y = sb("up_y", [P, 2, HID])
        dn_y = sb("dn_y", [P, 2, HID])
        row_y = sb("row_y", [1, 2, HID])
        bf_t = sb("bf_t", [P, 2, HID])
        wdn = sb("wdn", [P, HC, E])
        bup = sb("bup", [P, HC])

        x_all = sb("x_all", [P, TILES, E])
        stats = sb("stats", [P, KT, 6])
        mv = sb("mv", [P, KT, 2])
        veps = sb("veps", [P, KT])
        rstd = sb("rstd", [P, KT])

        qx = sb("qx", [P, 2, 2, HG, QH], BF16)
        kx = sb("kx", [P, 2, HG, N], BF16)
        vg = sb("vg", [P, 2, KT, HG, VW])
        pr = sb("pr", [P, 4, 2, QH])
        mx = sb("mx", [P, HG * QT, 2])
        negm = sb("negm", [P, HG * QT])
        mres = sb("mres", [P, HG * QT])
        mparts = sb("mparts", [P, MW], BF16)
        mrow = sb("mrow", [PARTS * HG * QT, P], BF16)
        osb = sb("osb", [P, 2, QH])

        xn = sb("xn", [P, KT, E])
        xt = sb("xt", [P, N])
        qkf = sb("qkf", [P, 2, N])
        qkr = sb("qkr", [P, 2, N])
        qkp = sb("qkp", [P, 2, PARTS, 2, N], BF16)
        vst = sb("vst", [P, 2, NG, KT, HG, VW])

        o_in = sb("o_in", [2 * HG * VW, 2, 2, TB])
        rec = sb("rec", [P, BT * H])
        att = sb("att", [P, BT, E])
        att_t = sb("att_t", [P, TB])
        yb = sb("yb", [P, BT, E])
        st3 = sb("st3", [P, BT, 6])
        mv3 = sb("mv3", [P, BT, 2])
        ve3 = sb("ve3", [P, BT])
        rs3 = sb("rs3", [P, BT])
        x1 = sb("x1", [P, 2, BT, E])
        x1n = sb("x1n", [P, BT, E])
        x1t = sb("x1t", [P, 2, TB])
        gt = qkf[:, :, :].rearrange("p w (c t) -> p (w c) t", t=TB)
        y2 = sb("y2", [P, BT, E])
        res = sb("res", [P, 2, BT, E])

        ps = ctx.enter_context(nc.psum_tensor("ps", [P, 8, 512], FP32))
        ps_bf = ps[:, 7, :].bitcast(BF16)

        w_attn_loaded = sem("w_attn_loaded")
        w_ffn_loaded = sem("w_ffn_loaded")
        x_loaded = [sem(f"x_loaded{s}") for s in range(2)]
        consts_ready = sem("consts_ready")
        ones_cleared = sem("ones_cleared")
        perm_ready = sem("perm_ready")
        setup_mm = sem("setup_mm")
        setup_copied = sem("setup_copied")
        stats_ready = sem("stats_ready")
        mv_ready = sem("mv_ready")
        veps_ready = sem("veps_ready")
        rstd_ready = sem("rstd_ready")
        xn_ready = sem("xn_ready")
        xt_mm = sem("xt_mm")
        xt_ready = sem("xt_ready")
        qkv_mm = sem("qkv_mm")
        qkf_ready = sem("qkf_ready")
        v_copied = sem("v_copied")
        part1_ready = sem("part1_ready")
        res1_ready = sem("res1_ready")
        part2_ready = sem("part2_ready")
        part3_ready = sem("part3_ready")
        parts_stored = [sem(f"parts_stored{s}") for s in range(2)]
        kq_loaded = [sem(f"kq_loaded{s}") for s in range(2)]
        v_loaded = [sem(f"v_loaded{s}") for s in range(2)]
        max_scores = sem("max_scores")
        max_read = sem("max_read")
        mchain = sem("mchain")
        m_transposed = sem("m_transposed")
        m_copied = sem("m_copied")
        m_rows_loaded = sem("m_rows_loaded")
        exp_scores = sem("exp_scores")
        exp_done = sem("exp_done")
        pv_done = sem("pv_done")
        o_cleared = sem("o_cleared")
        o_copied = sem("o_copied")
        o_stored = [sem(f"o_stored{s}") for s in range(2)]
        bf_loaded = [sem(f"bf_loaded{s}") for s in range(2)]
        bf_step = sem("bf_step")
        ffn_mm = sem("ffn_mm")
        ffn_w_ready = sem("ffn_w_ready")
        o_in_loaded = [sem(f"o_in_loaded{s}") for s in range(2)]
        o_tr = sem("o_tr")
        rec_ready = sem("rec_ready")
        att_ready = sem("att_ready")
        att_tr = sem("att_tr")
        att_t_ready = sem("att_t_ready")
        y_mm = sem("y_mm")
        dch = sem("dch")
        ln_mv = sem("ln_mv")
        ln_veps = sem("ln_veps")
        ln_rstd = sem("ln_rstd")
        x1n_ready = sem("x1n_ready")
        x1_tr = sem("x1_tr")
        x1t_ready = sem("x1t_ready")
        h_mm = sem("h_mm")
        gelu_done = sem("gelu_done")
        y2_mm = sem("y2_mm")
        y2_read = sem("y2_read")
        res_ready = sem("res_ready")
        vones_ready = sem("vones_ready")
        res_stored = [sem(f"res_stored{s}") for s in range(2)]

        block = ctx.enter_context(nc.Block())

        N_ATTN_W, N_FFN_W = 5, 6
        STORES = 2 * PARTS + 1
        KQ = 16 * (2 * PARTS + PARTS * PARTS)
        MROW = 16 * PARTS
        OST = 16 * HG
        CH = 5
        STEP_IT = 4 * STEPS
        TURNS = UNITS * STEPS // STEP_IT
        BF_STEPS = 3 * 3 * STAGES + 2

        @block.sync
        def _(sp):
            for b in range(2):
                sp.dma_start(x_all[:, b * KT:(b + 1) * KT, :],
                             x[b].rearrange("(t p) e -> p t e", p=P)).then_inc(x_loaded[b], 16)
            sp.dma_start(wqkv[:, :], w_qkv).then_inc(w_attn_loaded, 16)
            sp.dma_start(brow[:, :], b_qkv.rearrange("(o n) -> o n", o=1)).then_inc(w_attn_loaded, 16)
            sp.dma_start(bv[:, :], b_qkv[2 * E:].partition_broadcast(P)).then_inc(w_attn_loaded, 16)
            sp.dma_start(wout[:, :], w_out).then_inc(w_attn_loaded, 16)
            sp.dma_start(bout[:, :], b_out.partition_broadcast(P)).then_inc(w_attn_loaded, 16)
            for b in range(2):
                sp.wait_ge(x_loaded[b], 16)
                sp.dma_start(x_all[:, (b + 2) * KT:(b + 3) * KT, :],
                             x[b + 2].rearrange("(t p) e -> p t e", p=P)).then_inc(x_loaded[b], 16)

            with sp.Fori(0, B // 2) as it:
                for s in range(2):
                    bt = it * 2 + s
                    sp.wait_ge(part1_ready, bt + 1)
                    sp.wait_ge(part2_ready, bt + 1)
                    sp.wait_ge(part3_ready, bt + 1)
                    for w, dst in ((0, q_dram), (1, k_dram)):
                        for i in range(PARTS):
                            sp.dma_start(dst[bass.ds(bt * NG, NG), i, :, :],
                                         qkp[:, s, i, w, :]).then_inc(parts_stored[s], 16)
                    sp.wait_ge(v_copied, bt + 1)
                    sp.dma_start(v_dram[bass.ds(bt * NG, NG), :, :].rearrange("g p f -> p g f"),
                                 vst[:, s].rearrange("p g t h c -> p g (t h c)")).then_inc(parts_stored[s], 16)
            for s in range(2):
                sp.wait_ge(parts_stored[s], 16 * STORES * (B // 2))
            sp.wait_ge(ones_cleared, 1)

            def load_group(slot, group):
                for j in range(PARTS):
                    r = j * PARTS * D
                    for half in range(2):
                        sp.dma_start(qx[r:r + PARTS * D, slot, half, :, :],
                                     q_dram[bass.ds(group, 1), :, :, half * QH:(half + 1) * QH]
                                     .rearrange("o i (e h) t -> (o i e) h t", h=HG)).then_inc(kq_loaded[slot], 16)
                    for i in range(PARTS):
                        sp.dma_start(kx[r + i * D:r + (i + 1) * D, slot].rearrange("r h t -> r (h t)"),
                                     k_dram[bass.ds(group, 1), j].rearrange("o (e h) t -> (o e) (h t)", h=HG)
                                     ).then_inc(kq_loaded[slot], 16)

            def load_v(slot, group):
                sp.dma_start(vg[:, slot].rearrange("p t h c -> p (t h c)"),
                             v_dram[bass.ds(group, 1)].rearrange("o p f -> (o p) f")).then_inc(v_loaded[slot], 16)

            def load_m_rows(turn, du):
                sp.wait_ge(m_copied, turn * 4 + du + 1)
                slot, half = (du // 2) % 2, du % 2
                for i in range(PARTS):
                    sp.dma_start(qx[PROD + i:PROD + i + 1, slot, half, :, :].rearrange("o h t -> o (h t)"),
                                 mrow[i * HG * QT:(i + 1) * HG * QT, :]).then_inc(m_rows_loaded, 16)

            def store_o(turn, du):
                half = du % 2
                sp.wait_ge(o_copied, turn * 4 + du + 1)
                for h in range(HG):
                    sp.dma_start(o_dram[bass.ds(turn * 2 + du // 2, 1), half, h * VW:(h + 1) * VW, :]
                                 .rearrange("o c t -> (o c) t"),
                                 osb[32 * h:32 * h + VW, half, :]).then_inc(o_stored[half], 16)

            def turn_dmas(turn, last):
                load_m_rows(turn, 1)
                store_o(turn, 0)
                load_m_rows(turn, 2)
                if not last:
                    sp.wait_ge(exp_scores, turn * 2 * STEP_IT + STEP_IT)
                    load_group(0, turn * 2 + 2)
                store_o(turn, 1)
                if not last:
                    sp.wait_ge(pv_done, turn * STEP_IT + STEP_IT // 2)
                    load_v(0, turn * 2 + 2)
                load_m_rows(turn, 3)
                store_o(turn, 2)
                if not last:
                    load_m_rows(turn, 4)
                    sp.wait_ge(exp_scores, turn * 2 * STEP_IT + 2 * STEP_IT)
                    load_group(1, turn * 2 + 3)
                store_o(turn, 3)
                if not last:
                    sp.wait_ge(pv_done, turn * STEP_IT + STEP_IT)
                    load_v(1, turn * 2 + 3)

            load_group(0, 0)
            load_group(1, 1)
            load_v(0, 0)
            load_v(1, 1)
            load_m_rows(0, 0)
            with sp.Fori(0, TURNS - 1) as turn:
                turn_dmas(turn, False)
            turn_dmas(TURNS - 1, True)

            def load_o(bt, half):
                for j in range(2):
                    sp.dma_start(o_in[:, half, j, :],
                                 o_dram[bass.ds(bt * NG + 2 * j, 2), half, :, :]).then_inc(o_in_loaded[half], 16)

            def store_res(bt, half):
                sp.wait_ge(res_ready, bt * 2 + half + 1)
                sp.dma_start(out[bass.ds(bt, 1), half * TB:(half + 1) * TB, :]
                             .rearrange("o (t p) e -> p (o t) e", p=P), res[:, half, :, :]
                             ).then_inc(res_stored[half], 16)

            for half in range(2):
                sp.wait_ge(o_stored[half], OST * GROUPS)
            for half in range(2):
                load_o(0, half)
            with sp.Fori(0, B - 1) as bt:
                for half in range(2):
                    sp.wait_ge(o_tr, bt * 2 + half + 1)
                    load_o(bt + 1, half)
                    store_res(bt, half)
            for half in range(2):
                store_res(B - 1, half)
            for half in range(2):
                sp.wait_ge(res_stored[half], 16 * B)

        @block.gpsimd
        def _(pool):
            nc.gpsimd.memset(ident[:, :], 0.0).then_inc(consts_ready, 1)
            nc.gpsimd.memset(ident_bf[:, :], 0.0).then_inc(consts_ready, 1)
            nc.gpsimd.memset(one[:, :], 1.0).then_inc(consts_ready, 1)
            nc.gpsimd.memset(neghalf[:, :], -0.5).then_inc(consts_ready, 1)
            nc.gpsimd.memset(eps_c[:, :], EPS).then_inc(consts_ready, 1)
            nc.gpsimd.memset(mparts[:, PARTS * HG * QT:], 0.0).then_inc(consts_ready, 1)
            pool.wait_ge(consts_ready, 6)
            for m in (ident, ident_bf):
                nc.gpsimd.affine_select(out=m[:, :], in_=m[:, :], compare_op=ALU.not_equal, fill=1.0,
                                        base=0, pattern=[[-1, P]], channel_multiplier=1).then_inc(consts_ready, 1)
            nc.gpsimd.memset(vst[:, :, :, :, :, :].rearrange("p s g t h c -> p (s g t h c)"),
                             math.sqrt(E)).then_inc(vones_ready, 1)
            pool.wait_ge(vones_ready, 1)
            nc.gpsimd.memset(kx[64:96, :, :, :].rearrange("p s h t -> p (s h t)"), 1.0).then_inc(ones_cleared, 1)

            pool.wait_ge(ones_cleared, 1)
            with pool.Fori(0, B) as bt:
                pool.wait_ge(mv_ready, bt + 1)
                nc.gpsimd.tensor_tensor(veps[:, :], mv[:, :, 1], eps_c[:, :], ALU.add).then_inc(veps_ready, 1)
                pool.wait_ge(veps_ready, bt + 1)
                nc.gpsimd.tensor_tensor(rstd[:, :], veps[:, :], neghalf[:, :], ALU.pow).then_inc(rstd_ready, 1)

            steps = [0]

            def then(ins):
                ins.then_inc(bf_step, 1)
                steps[0] += 1
                pool.wait_ge(bf_step, steps[0])

            def butterfly(y_in, y_out, w, stride, rows, transposed):
                nb = HID // (2 * stride)
                y = y_in.rearrange("p (n r j) -> p n r j", r=2, j=stride)
                wv = w.rearrange("p (n j c) -> p n c j", j=stride, c=4)
                shape = [rows, nb, 2, stride]
                for r in range(2):
                    c = slice(2 * r, 2 * r + 2) if transposed else slice(r, r + 3, 2)
                    then(nc.gpsimd.tensor_tensor(
                        bf_t[0:rows, r, :].rearrange("p (n o j) -> p n o j", o=2, j=stride),
                        y[:, :, r:r + 1, :].to_broadcast(shape), wv[:, :, c, :], ALU.mult))
                then(nc.gpsimd.tensor_tensor(y_out, bf_t[0:rows, 0, :], bf_t[0:rows, 1, :], ALU.add))

            def load_stage(n):
                w, stage = (up_w, n) if n < STAGES else (down_w, 2 * STAGES - 1 - n)
                pool.dma_start(wst[:, n % 2, :],
                               w[stage].rearrange("k o i -> (k o i)").partition_broadcast(P)
                               ).then_inc(bf_loaded[n % 2], 16)

            load_stage(0)
            load_stage(1)
            pool.wait_ge(w_ffn_loaded, 16 * N_FFN_W)
            pool.wait_ge(setup_copied, 2)
            for n in range(2 * STAGES):
                pool.wait_ge(bf_loaded[n % 2], 16 * (n // 2 + 1))
                w = wst[:, n % 2, :]
                k = n % STAGES
                if n < STAGES:
                    butterfly(wexp[:, :] if k == 0 else up_y[:, (k + 1) % 2, :], up_y[:, k % 2, :], w,
                              2 ** k, P, False)
                    butterfly(bexp[:, :] if k == 0 else row_y[:, (k + 1) % 2, :], row_y[:, k % 2, :], w[0:1, :],
                              2 ** k, 1, False)
                else:
                    butterfly(dn_y[:, (k + 1) % 2, :], dn_y[:, k % 2, :], w, 2 ** (STAGES - 1 - k), P, True)
                if n + 2 < 2 * STAGES:
                    load_stage(n + 2)
            then(nc.gpsimd.tensor_tensor(row_y[:, 1, :], row_y[:, 0, :], upb[:, :], ALU.add))
            then(nc.gpsimd.tensor_tensor(bffn[:, :], bcon[:, :], bdown[:, :], ALU.add))
            assert steps[0] == BF_STEPS

            with pool.Fori(0, 3 * BLOCKS) as n:
                pool.wait_ge(ln_mv, n + 1)
                nc.gpsimd.tensor_tensor(ve3[:, :], mv3[:, :, 1], eps_c[:, 0:BT], ALU.add).then_inc(ln_veps, 1)
                pool.wait_ge(ln_veps, n + 1)
                nc.gpsimd.tensor_tensor(rs3[:, :], ve3[:, :], neghalf[:, 0:BT], ALU.pow).then_inc(ln_rstd, 1)

        @block.scalar
        def _(act):
            act.dma_start(wexp[:, :], w_exp).then_inc(w_ffn_loaded, 16)
            act.dma_start(wcon[:, :, :], w_con.rearrange("(c p) e -> p c e", p=P)).then_inc(w_ffn_loaded, 16)
            act.dma_start(bexp[:, :], b_exp.rearrange("(o n) -> o n", o=1)).then_inc(w_ffn_loaded, 16)
            act.dma_start(upb[:, :], up_b.rearrange("(o n) -> o n", o=1)).then_inc(w_ffn_loaded, 16)
            act.dma_start(bcon[:, :], b_con.partition_broadcast(P)).then_inc(w_ffn_loaded, 16)
            act.dma_start(bdown[:, :], down_b.partition_broadcast(P)).then_inc(w_ffn_loaded, 16)
            act.wait_ge(setup_mm, 2)
            nc.scalar.copy(dn_y[:, 1, :], ps[:, 1, :]).then_inc(setup_copied, 1)

            with act.Fori(0, B // 2) as it:
                for s in range(2):
                    bt = it * 2 + s
                    for b in range(2):
                        act.wait_ge(xt_mm, bt * 2 + b + 1)
                        nc.scalar.copy(xt[:, b * 512:(b + 1) * 512], ps[:, b, :]).then_inc(xt_ready, 1)
                    act.wait_ge(qkf_ready, bt + 1)
                    act.wait_ge(parts_stored[s], it * (16 * STORES))
                    nc.scalar.copy(qkp[:, s, 0, :, :], qkf[:, :, :]).then_inc(part1_ready, 1)
                    act.wait_ge(res1_ready, bt + 1)
                    nc.scalar.copy(qkp[:, s, 1, :, :], qkr[:, :, :]).then_inc(part2_ready, 1)

            def copy_o(turn, du):
                act.wait_ge(pv_done, turn * STEP_IT + STEPS * (du + 1))
                act.wait_ge(o_stored[du % 2], turn * (2 * OST) + (du // 2) * OST)
                nc.scalar.copy(osb[:, du % 2, :], ps[:, 6, :]).then_inc(o_copied, 1)

            def weights(turn):
                for s in range(STEP_IT):
                    if s % STEPS == 1 and s > 1:
                        copy_o(turn, s // STEPS - 1)
                    for j in range(2):
                        n = 2 * s + j
                        act.wait_ge(exp_scores, turn * 2 * STEP_IT + n + 1)
                        if j == 0:
                            act.wait_ge(pv_done, turn * STEP_IT + max(s - 1, 0))
                        nc.scalar.activation(pr[:, n % 4, :, :], ps[:, 2 + 2 * j:4 + 2 * j, :],
                                             ACT.Exp).then_inc(exp_done, 1)
                copy_o(turn, 3)

            act.wait_ge(o_cleared, 1)
            with act.Fori(0, TURNS - 1) as turn:
                weights(turn)
            weights(TURNS - 1)

            act.wait_ge(ffn_mm, 2)
            nc.scalar.copy(wdn[:, :, :], ps[:, 5, :]).then_inc(ffn_w_ready, 1)
            nc.scalar.copy(bup[:, :], ps[:, 6, 0:HC]).then_inc(ffn_w_ready, 1)
            act.wait_ge(ffn_w_ready, 2)

            def copy_att(t):
                act.wait_ge(att_tr, t + 1)
                nc.scalar.copy(att_t[:, :], ps[:, 2, :]).then_inc(att_t_ready, 1)

            def copy_x1(t, s):
                act.wait_ge(x1_tr, t + 1)
                nc.scalar.copy(x1t[:, s, :], ps[:, 4, :]).then_inc(x1t_ready, 1)

            def gelu(t, c):
                act.wait_ge(h_mm, t * HC + c + 1)
                nc.scalar.activation(gt[:, c, :], ps[:, 5 + c % 2, :], ACT.Gelu,
                                     bias=bup[:, c:c + 1]).then_inc(gelu_done, 1)

            def block_act(t, s, last):
                gelu(t, 0)
                gelu(t, 1)
                if not last:
                    copy_att(t + 1)
                gelu(t, 2)
                gelu(t, 3)
                if not last:
                    copy_x1(t + 1, 1 - s)

            copy_att(0)
            copy_x1(0, 0)
            with act.Fori(0, BLOCKS // 2 - 1) as i:
                for s in range(2):
                    block_act(i * 2 + s, s, False)
            block_act(BLOCKS - 2, 0, False)
            block_act(BLOCKS - 1, 1, True)

        @block.vector
        def _(dve):
            dve.wait_ge(w_attn_loaded, 16 * N_ATTN_W)
            for w in range(2):
                nc.vector.tensor_copy(wqk[:, w, :].rearrange("p (g e h) -> p g e h", e=D, h=HG),
                                      wqkv[:, w * E:(w + 1) * E].rearrange("p (g h e) -> p g e h", e=D, h=HG)
                                      ).then_inc(perm_ready, 1)
                nc.vector.tensor_copy(brow_qk[:, w, :].rearrange("p (g e h) -> p g e h", e=D, h=HG),
                                      brow[:, w * E:(w + 1) * E].rearrange("p (g h e) -> p g e h", e=D, h=HG)
                                      ).then_inc(perm_ready, 1)
            dve.wait_ge(setup_mm, 1)
            nc.vector.tensor_copy(bqk[:, :], ps[:, 0, 0:2]).then_inc(setup_copied, 1)

            dve.wait_ge(setup_copied, 2)
            dve.wait_ge(vones_ready, 1)
            with dve.Fori(0, B // 2) as it:
                for s in range(2):
                    bt = it * 2 + s
                    dve.wait_ge(x_loaded[s], (it + 1) * 16)
                    for t in range(KT):
                        last = nc.vector.bn_stats(stats[:, t, :],
                                                  x_all[:, bass.ds(bt * KT + t, 1), :].rearrange("p o e -> p (o e)"))
                    last.then_inc(stats_ready, 1)
                    dve.wait_ge(stats_ready, bt + 1)
                    nc.vector.tensor_copy(carrier[:, :], stats[:, 0, 0:1])
                    for t in range(KT):
                        last = nc.vector.bn_aggr(mv[:, t, :], stats[:, t, :])
                    last.then_inc(mv_ready, 1)
                    dve.wait_ge(rstd_ready, bt + 1)
                    dve.wait_ge(mv_ready, bt + 1)
                    for t in range(KT):
                        last = nc.vector.tensor_scalar(xn[:, t, :],
                                                       x_all[:, bass.ds(bt * KT + t, 1), :].rearrange("p o e -> p (o e)"),
                                                       mv[:, t, 0:1], rstd[:, t:t + 1], ALU.subtract, ALU.mult)
                    last.then_inc(xn_ready, 1)
                    dve.wait_ge(qkv_mm, bt * 2 + 1)
                    for w in range(2):
                        last = nc.vector.tensor_scalar_add(qkf[:, w, :].rearrange("p (b n) -> p b n", b=2),
                                                           ps[:, 2 + 2 * w:4 + 2 * w, :], bqk[:, w:w + 1])
                    last.then_inc(qkf_ready, 1)
                    dve.wait_ge(qkv_mm, bt * 2 + 2)
                    dve.wait_ge(parts_stored[s], it * (16 * STORES))
                    for t in range(KT):
                        last = nc.vector.tensor_tensor(
                            vst[:, s, :, t, :, 0:D],
                            ps[:, 6 + t // 4, (t % 4) * P:(t % 4 + 1) * P].rearrange("p (g h e) -> p g h e", h=HG, e=D),
                            bv[:, :].rearrange("p (g h e) -> p g h e", h=HG, e=D), ALU.add)
                    last.then_inc(v_copied, 1)
                    dve.wait_ge(part1_ready, bt + 1)
                    nc.vector.tensor_tensor(qkr[:, :, :], qkf[:, :, :], qkp[:, s, 0, :, :],
                                            ALU.subtract).then_inc(res1_ready, 1)
                    dve.wait_ge(part2_ready, bt + 1)
                    dve.wait_ge(res1_ready, bt + 1)
                    nc.vector.tensor_tensor(qkp[:, s, 2, :, :], qkr[:, :, :], qkp[:, s, 1, :, :],
                                            ALU.subtract).then_inc(part3_ready, 1)

            nc.vector.memset(ps[:, 6, :], 0.0).then_inc(o_cleared, 1)

            def split_maxima(turn, du):
                done = [turn * (4 * CH) + du * CH]

                def then(ins, wait=True):
                    ins.then_inc(mchain, 1)
                    done[0] = done[0] + 1
                    if wait:
                        dve.wait_ge(mchain, done[0])

                dve.wait_ge(max_read, (turn * 4 + du + 1) * (4 * STEPS))
                then(nc.vector.tensor_reduce(negm[:, :], mx[:, :, :], AX.X, ALU.max, negate=True))
                then(nc.vector.tensor_copy(mparts[:, 0 * HG * QT:1 * HG * QT], negm[:, :]))
                then(nc.vector.tensor_tensor(mres[:, :], negm[:, :], mparts[:, 0 * HG * QT:1 * HG * QT], ALU.subtract))
                then(nc.vector.tensor_copy(mparts[:, 1 * HG * QT:2 * HG * QT], mres[:, :]))
                then(nc.vector.tensor_tensor(mparts[:, 2 * HG * QT:3 * HG * QT], mres[:, :], mparts[:, 1 * HG * QT:2 * HG * QT], ALU.subtract), False)

            def copy_m(turn, du):
                dve.wait_ge(m_transposed, turn * 4 + du + 1)
                nc.vector.tensor_copy(mrow[:, :], ps_bf[0:PARTS * HG * QT, 0:P]).then_inc(m_copied, 1)

            def maxima(turn, c):
                r = c % STEPS
                for j in range(2):
                    for half in range(2):
                        dve.wait_ge(max_scores, turn * (4 * STEP_IT) + 4 * c + 2 * j + half + 1)
                        col = (r // 2) * QT + (r % 2) * 2 + j
                        nc.vector.tensor_reduce(mx[:, col, half:half + 1], ps[:, half, :], AX.X,
                                                ALU.max).then_inc(max_read, 1)
                if r == STEPS - 1:
                    split_maxima(turn, c // STEPS)
                if r == 0 and c > 0:
                    copy_m(turn, c // STEPS - 1)

            for c in range(LEAD):
                maxima(0, c)
            with dve.Fori(0, TURNS - 1) as turn:
                for s in range(STEP_IT):
                    maxima(turn, s + LEAD)
            for s in range(STEP_IT - LEAD):
                maxima(TURNS - 1, s + LEAD)
            copy_m(TURNS - 1, 3)

            def chain(base):
                done = [base]

                def then(ins):
                    ins.then_inc(dch, 1)
                    done[0] = done[0] + 1
                    dve.wait_ge(dch, done[0])
                return then

            def normalise(y, dst, then, n):
                for t in range(BT):
                    last = nc.vector.bn_stats(st3[:, t, :], y[:, t, :])
                then(last)
                nc.vector.tensor_copy(carrier[:, :], st3[:, 0, 0:1])
                for t in range(BT):
                    last = nc.vector.bn_aggr(mv3[:, t, :], st3[:, t, :])
                last.then_inc(ln_mv, 1)
                dve.wait_ge(ln_mv, n + 1)
                dve.wait_ge(ln_rstd, n + 1)
                for t in range(BT):
                    last = nc.vector.tensor_scalar(dst[:, t, :], y[:, t, :], mv3[:, t, 0:1], rs3[:, t:t + 1],
                                                   ALU.subtract, ALU.mult)
                return last

            def front(t, s, base, n):
                then = chain(base)
                dve.wait_ge(o_tr, t + 1)
                o = ps[:, 0:2, 0:2 * H * VW].rearrange("p k (t c) -> p k t c", c=VW)
                r = rec[:, :].rearrange("p (k t) -> p k t", k=2)
                then(nc.vector.reciprocal(r, o[:, :, :, D]))
                nc.vector.tensor_tensor(att[:, :, :].rearrange("p (k t) (h d) -> p k (t h) d", k=2, d=D),
                                        o[:, :, :, 0:D], r.unsqueeze(3).to_broadcast([P, 2, 2 * H, D]),
                                        ALU.mult).then_inc(att_ready, 1)
                dve.wait_ge(y_mm, t + 1)
                then(nc.vector.tensor_tensor(yb[:, :, :], ps[:, 3, :].rearrange("p (t e) -> p t e", e=E),
                                             bout[:, :].unsqueeze(1).to_broadcast([P, BT, E]), ALU.add))
                then(normalise(yb, yb, then, n))
                then(nc.vector.tensor_tensor(x1[:, s, :, :], yb[:, :, :], x_all[:, bass.ds(t * BT, BT), :],
                                             ALU.add))
                normalise(x1[:, s], x1n, then, n + 1).then_inc(x1n_ready, 1)

            def back(t, s, base, n, use):
                then = chain(base)
                dve.wait_ge(res_ready, t)
                dve.wait_ge(y2_mm, t + 1)
                ins = nc.vector.tensor_tensor(y2[:, :, :], ps[:, 7, :].rearrange("p (t e) -> p t e", e=E),
                                              bffn[:, :].unsqueeze(1).to_broadcast([P, BT, E]), ALU.add)
                ins.then_inc(y2_read, 1)
                dve.wait_ge(y2_read, t + 1)
                then(normalise(y2, y2, then, n))
                dve.wait_ge(res_stored[s], use * 16)
                nc.vector.tensor_tensor(res[:, s, :, :], y2[:, :, :], x1[:, s, :, :],
                                        ALU.add).then_inc(res_ready, 1)

            FRONT, BACK = 6, 2

            def block_dve(t, s, last, use):
                base = t * (FRONT + BACK) + FRONT
                if not last:
                    front(t + 1, 1 - s, base, t * 3 + 2)
                    back(t, s, base + FRONT, t * 3 + 4, use)
                else:
                    back(t, s, base, t * 3 + 2, use)

            front(0, 0, 0, 0)
            dve.wait_ge(bf_step, BF_STEPS)
            with dve.Fori(0, BLOCKS // 2 - 1) as i:
                for s in range(2):
                    block_dve(i * 2 + s, s, False, i)
            block_dve(BLOCKS - 2, 0, False, BLOCKS // 2 - 1)
            block_dve(BLOCKS - 1, 1, True, BLOCKS // 2 - 1)

        @block.tensor
        def _(pe):
            pe.wait_ge(perm_ready, 4)
            pe.wait_ge(consts_ready, 8)
            for w in range(2):
                last = nc.tensor.matmul(ps[:, 0, w:w + 1], brow_qk[0:1, w, :], one[:, :], start=True, stop=True)
            last.then_inc(setup_mm, 1)
            pe.wait_ge(w_ffn_loaded, 16 * N_FFN_W)
            for c in range(HC):
                last = nc.tensor.transpose(ps[:, 1, c * P:(c + 1) * P], wcon[:, c, :], ident[:, :])
            last.then_inc(setup_mm, 1)
            pe.wait_ge(setup_copied, 2)

            with pe.Fori(0, B) as bt:
                pe.wait_ge(xn_ready, bt + 1)
                for t in range(KT):
                    last = nc.tensor.transpose(ps[:, t // 4, (t % 4) * P:(t % 4 + 1) * P], xn[:, t, :], ident[:, :])
                    if t % 4 == 3:
                        last.then_inc(xt_mm, 1)
                pe.wait_ge(xt_ready, bt * 2 + 2)
                pe.wait_ge(qkf_ready, bt)
                for w in range(2):
                    for b in range(2):
                        last = nc.tensor.matmul(ps[:, 2 + 2 * w + b, :], wqk[:, w, :], xt[:, b * 512:(b + 1) * 512],
                                                start=True, stop=True)
                last.then_inc(qkv_mm, 1)
                pe.wait_ge(v_copied, bt)
                for t in range(KT):
                    last = nc.tensor.matmul(ps[:, 6 + t // 4, (t % 4) * P:(t % 4 + 1) * P],
                                            xt[:, t * P:(t + 1) * P], wqkv[:, 2 * E:3 * E], start=True, stop=True)
                last.then_inc(qkv_mm, 1)
            pe.wait_ge(qkf_ready, B)
            pe.wait_ge(v_copied, B)
            pe.wait_ge(o_cleared, 1)

            def transpose_m(turn, du):
                pe.wait_ge(mchain, turn * (4 * CH) + (du + 1) * CH)
                nc.tensor.transpose(ps_bf[0:MW, 0:P], mparts[:, :],
                                    ident_bf[:, :]).then_inc(m_transposed, 1)

            def max_tile(turn, c, j):
                r, slot = c % STEPS, (c // (2 * STEPS)) % 2
                if c % (2 * STEPS) == 0 and j == 0:
                    pe.wait_ge(kq_loaded[slot], (turn + c // STEP_IT + 1) * KQ)
                h, qt = r // 2, (r % 2) * 2 + j
                qhalf = (c // STEPS) % 2
                for half in range(2):
                    n = 4 * c + 2 * j + half
                    if n > 1:
                        pe.wait_ge(max_read, turn * (4 * STEP_IT) + n - 1)
                    nc.tensor.matmul(ps[:, half, :], qx[0:PROD, slot, qhalf, h, qt * P:(qt + 1) * P],
                                     kx[0:PROD, slot, h, half * 512:(half + 1) * 512],
                                     start=True, stop=True).then_inc(max_scores, 1)
                if r == 0 and j == 1 and c > 0:
                    transpose_m(turn, c // STEPS - 1)

            def score_pair(turn, s, j):
                slot, half, kt = s // (2 * STEPS), s // STEPS % 2, s % STEPS
                if kt == 0 and j == 0:
                    pe.wait_ge(m_rows_loaded, (turn * 4 + s // STEPS + 1) * MROW)
                pe.wait_ge(exp_done, turn * (2 * STEP_IT) + max(2 * s + j - 1, 0))
                for h in range(2):
                    last = nc.tensor.matmul(ps[:, 2 + 2 * j + h, :], kx[0:ROWS, slot, 2 * j + h, kt * P:(kt + 1) * P],
                                            qx[0:ROWS, slot, half, 2 * j + h, :],
                                            start=True, stop=True)
                last.then_inc(exp_scores, 1)

            def weigh_v(turn, s):
                slot, kt = s // (2 * STEPS), s % STEPS
                pe.wait_ge(exp_done, turn * (2 * STEP_IT) + 2 * s + 2)
                if s % (2 * STEPS) == 0:
                    pe.wait_ge(v_loaded[slot], (turn + 1) * 16)
                if kt == 0:
                    pe.wait_ge(o_copied, turn * 4 + s // STEPS)
                for h in range(HG):
                    last = nc.tensor.matmul(ps[32 * h:32 * h + VW, 6, :], vg[:, slot, kt, h, :],
                                            pr[:, 2 * (s % 2) + h // 2, h % 2, :],
                                            start=(kt == 0), stop=(kt == STEPS - 1))
                last.then_inc(pv_done, 1)

            def turn_pe(turn, last_turn):
                for s in range(STEP_IT):
                    ahead = not last_turn or s + LEAD < STEP_IT
                    end = s == STEP_IT - 1
                    score_pair(turn, s, 0)
                    if ahead and not end:
                        max_tile(turn, s + LEAD, 0)
                    score_pair(turn, s, 1)
                    if ahead and not end:
                        max_tile(turn, s + LEAD, 1)
                    if last_turn and s + LEAD == STEP_IT:
                        transpose_m(turn, 3)
                    if s > 0:
                        weigh_v(turn, s - 1)
                    if ahead and end:
                        max_tile(turn, s + LEAD, 0)
                        max_tile(turn, s + LEAD, 1)
                weigh_v(turn, STEP_IT - 1)

            for c in range(LEAD):
                max_tile(0, c, 0)
                max_tile(0, c, 1)
            with pe.Fori(0, TURNS - 1) as turn:
                turn_pe(turn, False)
            turn_pe(TURNS - 1, True)

            pe.wait_ge(bf_step, BF_STEPS)
            pe.wait_ge(exp_done, 2 * STEP_IT * TURNS)
            pe.wait_ge(o_copied, UNITS)
            pe.wait_ge(max_read, 4 * STEP_IT * TURNS)
            pe.wait_ge(m_copied, UNITS)
            for c in range(HC):
                last = nc.tensor.transpose(ps[:, 5, c * P:(c + 1) * P], dn_y[:, 0, c * P:(c + 1) * P], ident[:, :])
            last.then_inc(ffn_mm, 1)
            for c in range(HC):
                last = nc.tensor.matmul(ps[:, 6, c:c + 1], row_y[0:1, 1, c * P:(c + 1) * P], one[:, :],
                                        start=True, stop=True)
            last.then_inc(ffn_mm, 1)

            def untranspose(t, s, use):
                pe.wait_ge(o_in_loaded[s], (use + 1) * 32)
                rows = 2 * HG * VW
                for tt in range(BT):
                    for j in range(2):
                        c = (tt % 2) * 2 * rows + j * rows
                        last = nc.tensor.transpose(ps[:, tt // 2, c:c + rows], o_in[:, s, j, tt * P:(tt + 1) * P],
                                                   ident[0:rows, 0:rows])
                last.then_inc(o_tr, 1)

            def transpose_att(t):
                pe.wait_ge(att_ready, t + 1)
                for tt in range(BT):
                    last = nc.tensor.transpose(ps[:, 2, tt * P:(tt + 1) * P], att[:, tt, :], ident[:, :])
                last.then_inc(att_tr, 1)

            def project_out(t):
                pe.wait_ge(att_t_ready, t + 1)
                for tt in range(BT):
                    last = nc.tensor.matmul(ps[:, 3, tt * P:(tt + 1) * P], att_t[:, tt * P:(tt + 1) * P], wout[:, :],
                                            start=True, stop=True)
                last.then_inc(y_mm, 1)

            def transpose_x1(t):
                pe.wait_ge(x1n_ready, t + 1)
                for tt in range(BT):
                    last = nc.tensor.transpose(ps[:, 4, tt * P:(tt + 1) * P], x1n[:, tt, :], ident[:, :])
                last.then_inc(x1_tr, 1)

            def hidden(t, s, c):
                if c == 0:
                    pe.wait_ge(x1t_ready, t + 1)
                pe.wait_ge(gelu_done, t * HC + max(c - 1, 0))
                nc.tensor.matmul(ps[:, 5 + c % 2, :], up_y[:, 0, c * P:(c + 1) * P], x1t[:, s, :],
                                 start=True, stop=True).then_inc(h_mm, 1)

            def contract(t):
                pe.wait_ge(gelu_done, t * HC + HC)
                pe.wait_ge(y2_read, t)
                for tt in range(BT):
                    for c in range(HC):
                        last = nc.tensor.matmul(ps[:, 7, tt * P:(tt + 1) * P], gt[:, c, tt * P:(tt + 1) * P],
                                                wdn[:, c, :], start=(c == 0), stop=(c == HC - 1))
                last.then_inc(y2_mm, 1)

            def block_pe(t, s, last, use):
                if not last:
                    untranspose(t + 1, 1 - s, use)
                hidden(t, s, 0)
                hidden(t, s, 1)
                if not last:
                    transpose_att(t + 1)
                hidden(t, s, 2)
                hidden(t, s, 3)
                if not last:
                    project_out(t + 1)
                contract(t)
                if not last:
                    transpose_x1(t + 1)

            untranspose(0, 0, 0)
            transpose_att(0)
            project_out(0)
            transpose_x1(0)
            pe.wait_ge(ffn_w_ready, 2)
            with pe.Fori(0, BLOCKS // 2 - 1) as i:
                block_pe(i * 2, 0, False, i)
                block_pe(i * 2 + 1, 1, False, i + 1)
            block_pe(BLOCKS - 2, 0, False, BLOCKS // 2 - 1)
            block_pe(BLOCKS - 1, 1, True, 0)

    return nc


NAMES = ["L0_attn_x", "L0_attn_W_qkv", "L0_attn_b_qkv", "L0_attn_W_out", "L0_attn_b_out", "L0_ffn_W_exp",
         "L0_ffn_b_exp", "L0_ffn_up_weights", "L0_ffn_up_bias", "L0_ffn_down_weights", "L0_ffn_W_con",
         "L0_ffn_b_con", "L0_ffn_down_bias"]


def kernel(**inputs):
    import concourse.bacc as bacc
    from concourse.bass_utils import run_bass_kernel_spmd

    nc = bacc.Bacc("TRN2", target_bir_lowering=False, num_devices=1)
    arrays, args = {}, []
    for name in NAMES:
        a = np.ascontiguousarray(inputs[name])
        arrays[name] = a
        args.append(nc.dram_tensor(name, a.shape, mybir.dt.from_np(a.dtype), kind="ExternalInput").ap())
    out = nc.dram_tensor("out", (B, N, E), FP32, kind="ExternalOutput").ap()
    attention_ffn_kernel(nc, *args, out)
    got = run_bass_kernel_spmd(nc, [arrays], core_ids=[0])
    return got.results[0]["out"]
```

```python
import math
from contextlib import ExitStack

import numpy as np

import concourse.bass as bass
from concourse import mybir

FP32 = mybir.dt.float32
BF16 = mybir.dt.bfloat16
ALU = mybir.AluOpType
ACT = mybir.ActivationFunctionType
AX = mybir.AxisListType

P = 128
B, N, E = 4, 1024, 128
H = 16
D = E // H
HG = 4
NG = H // HG
GROUPS = B * NG
KT = N // P
TILES = B * KT
QH = N // 2
QT = QH // P
UNITS = GROUPS * 2
PARTS = 3
PROD = PARTS * PARTS * D
ROWS = PROD + PARTS
VW = D + 1
HID = 512
HC = HID // P
STAGES = int(math.log2(HID))
EPS = 1e-5
ROT = (0, 1, 7)
MW = 96
LEAD = 12
STEPS = KT
TB = 512
BT = TB // P
BLOCKS = B * N // TB


def attention_ffn_kernel(nc, x, w_qkv, b_qkv, w_out, b_out, w_exp, b_exp, up_w, up_b, down_w,
                         w_con, b_con, down_b, out):
    q_dram = nc.dram_tensor("q_parts", (GROUPS, PARTS, D * HG, N), BF16, kind="Internal").ap()
    k_dram = nc.dram_tensor("k_parts", (GROUPS, PARTS, D * HG, N), BF16, kind="Internal").ap()
    v_dram = nc.dram_tensor("v_ones", (GROUPS, P, KT * HG * VW), FP32, kind="Internal").ap()
    o_dram = nc.dram_tensor("o_sums", (GROUPS, 2, HG * VW, QH), FP32, kind="Internal").ap()

    ctx = ExitStack()
    with ctx:
        def sb(name, shape, dt=FP32):
            return ctx.enter_context(nc.sbuf_tensor(name, shape, dt))

        def sem(name):
            return ctx.enter_context(nc.semaphore(name))

        wqkv = sb("wqkv", [P, 3 * E])
        wqk = sb("wqk", [P, 2, E])
        brow = sb("brow", [1, 3 * E])
        brow_qk = sb("brow_qk", [1, 2, E])
        bqk = sb("bqk", [P, 2])
        bv = sb("bv", [P, E])
        wout = sb("wout", [P, E])
        bout = sb("bout", [P, E])
        wexp = sb("wexp", [P, HID])
        wcon = sb("wcon", [P, HC, E])
        bexp = sb("bexp", [1, HID])
        upb = sb("upb", [1, HID])
        bcon = sb("bcon", [P, E])
        bdown = sb("bdown", [P, E])
        bffn = sb("bffn", [P, E])
        ident = sb("ident", [P, P])
        ident_bf = sb("ident_bf", [P, P], BF16)
        one = sb("one", [1, 1])
        neghalf = sb("neghalf", [P, KT])
        eps_c = sb("eps_c", [P, KT])
        carrier = sb("carrier", [P, 1])

        wst = sb("wst", [P, 2, 4 * HID // 2])
        up_y = sb("up_y", [P, 2, HID])
        dn_y = sb("dn_y", [P, 2, HID])
        row_y = sb("row_y", [1, 2, HID])
        bf_t = sb("bf_t", [P, 2, HID])
        wdn = sb("wdn", [P, HC, E])
        bup = sb("bup", [P, HC])

        x_all = sb("x_all", [P, TILES, E])
        stats = sb("stats", [P, KT, 6])
        mv = sb("mv", [P, 2, KT, 2])
        veps = sb("veps", [P, KT])
        rstd = sb("rstd", [P, 2, KT])

        qx = sb("qx", [P, 2, 2, HG, QH], BF16)
        kx = sb("kx", [P, 2, HG, N], BF16)
        vg = sb("vg", [P, 2, KT, HG, VW])
        pr = sb("pr", [P, 4, 2, QH])
        mx = sb("mx", [P, 2, HG * QT, 2])
        negm = sb("negm", [P, HG * QT])
        mres = sb("mres", [P, HG * QT])
        mparts = sb("mparts", [P, MW], BF16)
        mrow = sb("mrow", [PARTS * HG * QT, P], BF16)

        xn = sb("xn", [P, KT, E])
        xt = sb("xt", [P, N])
        qkf = sb("qkf", [P, 2, N])
        qkr = sb("qkr", [P, 2, N])
        osb = qkr[:, :, :].rearrange("p w (c t) -> p (w c) t", t=QH)
        qkp = sb("qkp", [P, 2, PARTS, 2, N], BF16)
        vst = sb("vst", [P, 2, NG, KT, HG, VW])

        o_in = sb("o_in", [2 * HG * VW, 2, 2, TB])
        rec = sb("rec", [P, BT * H])
        att = sb("att", [P, BT, E])
        att_t = sb("att_t", [P, TB])
        yb = sb("yb", [P, BT, E])
        st3 = sb("st3", [P, BT, 6])
        mv3 = sb("mv3", [P, BT, 2])
        ve3 = sb("ve3", [P, BT])
        rs3 = sb("rs3", [P, BT])
        x1 = sb("x1", [P, 2, BT, E])
        x1n = sb("x1n", [P, BT, E])
        x1t = sb("x1t", [P, 2, TB])
        gt = qkf[:, :, :].rearrange("p w (c t) -> p (w c) t", t=TB)
        y2 = sb("y2", [P, BT, E])

        ps = ctx.enter_context(nc.psum_tensor("ps", [P, 8, 512], FP32))

        w_attn_loaded = sem("w_attn_loaded")
        w_ffn_loaded = sem("w_ffn_loaded")
        w_out_loaded = sem("w_out_loaded")
        x_loaded = [sem(f"x_loaded{b}") for b in range(B)]
        consts_ready = sem("consts_ready")
        ones_cleared = sem("ones_cleared")
        perm_ready = sem("perm_ready")
        setup_mm = sem("setup_mm")
        setup_copied = sem("setup_copied")
        stats_ready = sem("stats_ready")
        mv_ready = sem("mv_ready")
        veps_ready = sem("veps_ready")
        rstd_ready = sem("rstd_ready")
        xn_ready = sem("xn_ready")
        xt_mm = sem("xt_mm")
        xt_ready = sem("xt_ready")
        qk_mm = sem("qk_mm")
        v_mm = sem("v_mm")
        qkf_ready = sem("qkf_ready")
        v_copied = sem("v_copied")
        part1_ready = sem("part1_ready")
        res1_ready = sem("res1_ready")
        part2_ready = sem("part2_ready")
        part3_ready = sem("part3_ready")
        parts_stored = [sem(f"parts_stored{s}") for s in range(2)]
        kq_loaded = [sem(f"kq_loaded{s}") for s in range(2)]
        v_loaded = [sem(f"v_loaded{s}") for s in range(2)]
        max_scores = sem("max_scores")
        max_read = sem("max_read")
        mchain = sem("mchain")
        m_rows_loaded = sem("m_rows_loaded")
        exp_scores = sem("exp_scores")
        exp_done = sem("exp_done")
        pv_done = sem("pv_done")
        o_bank_free = sem("o_bank_free")
        o_stored = [sem(f"o_stored{s}") for s in range(2)]
        bf_loaded = [sem(f"bf_loaded{s}") for s in range(2)]
        bf_step = sem("bf_step")
        ffn_mm = sem("ffn_mm")
        ffn_w_ready = sem("ffn_w_ready")
        o_in_loaded = [sem(f"o_in_loaded{s}") for s in range(2)]
        o_tr = sem("o_tr")
        rec_ready = sem("rec_ready")
        att_ready = sem("att_ready")
        att_tr = sem("att_tr")
        att_t_ready = sem("att_t_ready")
        y_mm = sem("y_mm")
        dch = sem("dch")
        ln_mv = sem("ln_mv")
        ln_veps = sem("ln_veps")
        ln_rstd = sem("ln_rstd")
        x1n_ready = sem("x1n_ready")
        x1_tr = sem("x1_tr")
        x1t_ready = sem("x1t_ready")
        h_mm = sem("h_mm")
        gelu_done = sem("gelu_done")
        y2_mm = sem("y2_mm")
        y2_read = sem("y2_read")
        res_ready = sem("res_ready")
        vones_ready = sem("vones_ready")
        res_stored = [sem(f"res_stored{s}") for s in range(2)]

        block = ctx.enter_context(nc.Block())

        N_ATTN_W, N_FFN_W = 3, 6
        STORES = 2 * PARTS + 1
        KQ = 16 * (2 * PARTS + PARTS * PARTS)
        MROW = 16 * PARTS
        OST = 16 * HG
        CH = 5
        STEP_IT = 4 * STEPS
        TURNS = UNITS * STEPS // STEP_IT
        TURN_FILLS = 4 * (4 * STEPS + 1)
        assert TURN_FILLS % len(ROT) == 0
        BF_STEPS = 3 * 3 * STAGES + 2

        def fill_of(c, k):
            return 4 * c + k + (max(c - 2, 0) // STEPS)

        def fill_of_m(u, last=False):
            return fill_of(u * STEPS + STEPS - 1, 3) + 1 + (0 if last else 8)

        @block.sync
        def _(sp):
            for b in range(B):
                sp.dma_start(x_all[:, b * KT:(b + 1) * KT, :],
                             x[b].rearrange("(t p) e -> p t e", p=P)).then_inc(x_loaded[b], 16)
            sp.dma_start(wout[:, :], w_out).then_inc(w_out_loaded, 16)
            sp.dma_start(bout[:, :], b_out.partition_broadcast(P)).then_inc(w_out_loaded, 16)

            def load_group(slot, group):
                for j in range(PARTS):
                    r = j * PARTS * D
                    for half in range(2):
                        sp.dma_start(qx[r:r + PARTS * D, slot, half, :, :],
                                     q_dram[bass.ds(group, 1), :, :, half * QH:(half + 1) * QH]
                                     .rearrange("o i (e h) t -> (o i e) h t", h=HG)).then_inc(kq_loaded[slot], 16)
                    for i in range(PARTS):
                        sp.dma_start(kx[r + i * D:r + (i + 1) * D, slot].rearrange("r h t -> r (h t)"),
                                     k_dram[bass.ds(group, 1), j].rearrange("o (e h) t -> (o e) (h t)", h=HG)
                                     ).then_inc(kq_loaded[slot], 16)

            def load_v(slot, group):
                sp.dma_start(vg[:, slot].rearrange("p t h c -> p (t h c)"),
                             v_dram[bass.ds(group, 1)].rearrange("o p f -> (o p) f")).then_inc(v_loaded[slot], 16)

            def load_m_rows(turn, du, last=False):
                sp.wait_ge(max_read, turn * TURN_FILLS + fill_of_m(du, last) + 1)
                slot, half = (du // 2) % 2, du % 2
                for i in range(PARTS):
                    sp.dma_start(qx[PROD + i:PROD + i + 1, slot, half, :, :].rearrange("o h t -> o (h t)"),
                                 mrow[i * HG * QT:(i + 1) * HG * QT, :]).then_inc(m_rows_loaded, 16)

            def store_o(turn, du):
                half = du % 2
                sp.wait_ge(o_bank_free, turn * 4 + du + 2)
                for h in range(HG):
                    sp.dma_start(o_dram[bass.ds(turn * 2 + du // 2, 1), half, h * VW:(h + 1) * VW, :]
                                 .rearrange("o c t -> (o c) t"),
                                 osb[32 * h:32 * h + VW, du, :]).then_inc(o_stored[half], 16)

            def turn_dmas(turn, last):
                load_m_rows(turn, 1)
                store_o(turn, 0)
                load_m_rows(turn, 2)
                if not last:
                    sp.wait_ge(exp_scores, turn * 2 * STEP_IT + STEP_IT)
                    load_group(0, turn * 2 + 2)
                store_o(turn, 1)
                if not last:
                    sp.wait_ge(pv_done, turn * STEP_IT + STEP_IT // 2)
                    load_v(0, turn * 2 + 2)
                load_m_rows(turn, 3, last)
                store_o(turn, 2)
                if not last:
                    load_m_rows(turn, 4)
                    sp.wait_ge(exp_scores, turn * 2 * STEP_IT + 2 * STEP_IT)
                    load_group(1, turn * 2 + 3)
                store_o(turn, 3)
                if not last:
                    sp.wait_ge(pv_done, turn * STEP_IT + STEP_IT)
                    load_v(1, turn * 2 + 3)

            def store_parts(b):
                s = b % 2
                for i, ready in enumerate((part1_ready, part2_ready, part3_ready)):
                    sp.wait_ge(ready, b + 1)
                    for w, dst in ((0, q_dram), (1, k_dram)):
                        sp.dma_start(dst[b * NG:(b + 1) * NG, i, :, :], qkp[:, s, i, w, :]
                                     ).then_inc(parts_stored[s], 16)
                    if i == 0:
                        sp.wait_ge(v_copied, b + 1)
                        sp.dma_start(v_dram[b * NG:(b + 1) * NG, :, :].rearrange("g p f -> p g f"),
                                     vst[:, s].rearrange("p g t h c -> p g (t h c)")).then_inc(parts_stored[s], 16)

            store_parts(0)
            store_parts(1)
            sp.wait_ge(ones_cleared, 1)
            sp.wait_ge(parts_stored[0], 16 * STORES)
            for slot in range(2):
                load_group(slot, slot)
                load_v(slot, slot)
            store_parts(2)
            store_parts(3)
            for s in range(2):
                sp.wait_ge(parts_stored[s], 16 * STORES * (B // 2))
            load_m_rows(0, 0)
            with sp.Fori(0, TURNS - 1) as turn:
                turn_dmas(turn, False)
            turn_dmas(TURNS - 1, True)

            def load_o(bt, half):
                for j in range(2):
                    sp.dma_start(o_in[:, half, j, :],
                                 o_dram[bass.ds(bt * NG + 2 * j, 2), half, :, :]).then_inc(o_in_loaded[half], 16)

            def store_res(bt, half):
                sp.wait_ge(res_ready, bt * 2 + half + 1)
                sp.dma_start(out[bass.ds(bt, 1), half * TB:(half + 1) * TB, :]
                             .rearrange("o (t p) e -> p (o t) e", p=P),
                             x_all[:, bass.ds((bt * 2 + half) * BT, BT), :]
                             ).then_inc(res_stored[half], 16)

            for half in range(2):
                sp.wait_ge(o_stored[half], OST * GROUPS)
            for half in range(2):
                load_o(0, half)
            with sp.Fori(0, B - 1) as bt:
                for half in range(2):
                    sp.wait_ge(o_tr, bt * 2 + half + 1)
                    load_o(bt + 1, half)
                    store_res(bt, half)
            for half in range(2):
                store_res(B - 1, half)
            for half in range(2):
                sp.wait_ge(res_stored[half], 16 * B)

        @block.gpsimd
        def _(pool):
            nc.gpsimd.memset(ident[:, :], 0.0).then_inc(consts_ready, 1)
            nc.gpsimd.memset(ident_bf[:, :], 0.0).then_inc(consts_ready, 1)
            nc.gpsimd.memset(one[:, :], 1.0).then_inc(consts_ready, 1)
            nc.gpsimd.memset(neghalf[:, :], -0.5).then_inc(consts_ready, 1)
            nc.gpsimd.memset(eps_c[:, :], EPS).then_inc(consts_ready, 1)
            nc.gpsimd.memset(mparts[:, PARTS * HG * QT:], 0.0).then_inc(consts_ready, 1)
            pool.wait_ge(consts_ready, 6)
            for m in (ident, ident_bf):
                nc.gpsimd.affine_select(out=m[:, :], in_=m[:, :], compare_op=ALU.not_equal, fill=1.0,
                                        base=0, pattern=[[-1, P]], channel_multiplier=1).then_inc(consts_ready, 1)
            nc.gpsimd.memset(vst[:, :, :, :, :, :].rearrange("p s g t h c -> p (s g t h c)"),
                             math.sqrt(E)).then_inc(vones_ready, 1)
            pool.wait_ge(vones_ready, 1)
            nc.gpsimd.memset(kx[64:96, :, :, :].rearrange("p s h t -> p (s h t)"), 1.0).then_inc(ones_cleared, 1)

            pool.wait_ge(ones_cleared, 1)
            def batch_rstd(b):
                pool.wait_ge(mv_ready, b + 1)
                nc.gpsimd.tensor_tensor(veps[:, :], mv[:, b % 2, :, 1], eps_c[:, :], ALU.add).then_inc(veps_ready, 1)
                pool.wait_ge(veps_ready, b + 1)
                if b > 1:
                    pool.wait_ge(xn_ready, b - 1)
                nc.gpsimd.tensor_tensor(rstd[:, b % 2, :], veps[:, :], neghalf[:, :], ALU.pow).then_inc(rstd_ready, 1)

            batch_rstd(0)
            for b in range(B):
                if b + 1 < B:
                    batch_rstd(b + 1)
                pool.wait_ge(part2_ready, b + 1)
                if b > 0:
                    pool.wait_ge(part3_ready, b)
                nc.gpsimd.tensor_tensor(qkp[:, b % 2, 2, :, :], qkr[:, :, :], qkp[:, b % 2, 1, :, :],
                                        ALU.subtract).then_inc(part3_ready, 1)

            steps = [0]

            def then(ins):
                ins.then_inc(bf_step, 1)
                steps[0] += 1
                pool.wait_ge(bf_step, steps[0])

            def butterfly(y_in, y_out, w, stride, rows, transposed):
                nb = HID // (2 * stride)
                y = y_in.rearrange("p (n r j) -> p n r j", r=2, j=stride)
                wv = w.rearrange("p (n j c) -> p n c j", j=stride, c=4)
                shape = [rows, nb, 2, stride]
                for r in range(2):
                    c = slice(2 * r, 2 * r + 2) if transposed else slice(r, r + 3, 2)
                    then(nc.gpsimd.tensor_tensor(
                        bf_t[0:rows, r, :].rearrange("p (n o j) -> p n o j", o=2, j=stride),
                        y[:, :, r:r + 1, :].to_broadcast(shape), wv[:, :, c, :], ALU.mult))
                then(nc.gpsimd.tensor_tensor(y_out, bf_t[0:rows, 0, :], bf_t[0:rows, 1, :], ALU.add))

            def load_stage(n):
                w, stage = (up_w, n) if n < STAGES else (down_w, 2 * STAGES - 1 - n)
                pool.dma_start(wst[:, n % 2, :],
                               w[stage].rearrange("k o i -> (k o i)").partition_broadcast(P)
                               ).then_inc(bf_loaded[n % 2], 16)

            load_stage(0)
            load_stage(1)
            pool.wait_ge(w_ffn_loaded, 16 * N_FFN_W)
            pool.wait_ge(setup_copied, 2)
            for n in range(2 * STAGES):
                pool.wait_ge(bf_loaded[n % 2], 16 * (n // 2 + 1))
                w = wst[:, n % 2, :]
                k = n % STAGES
                if n < STAGES:
                    butterfly(wexp[:, :] if k == 0 else up_y[:, (k + 1) % 2, :], up_y[:, k % 2, :], w,
                              2 ** k, P, False)
                    butterfly(bexp[:, :] if k == 0 else row_y[:, (k + 1) % 2, :], row_y[:, k % 2, :], w[0:1, :],
                              2 ** k, 1, False)
                else:
                    butterfly(dn_y[:, (k + 1) % 2, :], dn_y[:, k % 2, :], w, 2 ** (STAGES - 1 - k), P, True)
                if n + 2 < 2 * STAGES:
                    load_stage(n + 2)
            then(nc.gpsimd.tensor_tensor(row_y[:, 1, :], row_y[:, 0, :], upb[:, :], ALU.add))
            then(nc.gpsimd.tensor_tensor(bffn[:, :], bcon[:, :], bdown[:, :], ALU.add))
            assert steps[0] == BF_STEPS

            with pool.Fori(0, 3 * BLOCKS) as n:
                pool.wait_ge(ln_mv, n + 1)
                nc.gpsimd.tensor_tensor(ve3[:, :], mv3[:, :, 1], eps_c[:, 0:BT], ALU.add).then_inc(ln_veps, 1)
                pool.wait_ge(ln_veps, n + 1)
                nc.gpsimd.tensor_tensor(rs3[:, :], ve3[:, :], neghalf[:, 0:BT], ALU.pow).then_inc(ln_rstd, 1)

        @block.scalar
        def _(act):
            act.dma_start(brow[:, :], b_qkv.rearrange("(o n) -> o n", o=1)).then_inc(w_attn_loaded, 16)
            act.dma_start(wqkv[:, :], w_qkv).then_inc(w_attn_loaded, 16)
            act.dma_start(bv[:, :], b_qkv[2 * E:].partition_broadcast(P)).then_inc(w_attn_loaded, 16)
            act.dma_start(wexp[:, :], w_exp).then_inc(w_ffn_loaded, 16)
            act.dma_start(wcon[:, :, :], w_con.rearrange("(c p) e -> p c e", p=P)).then_inc(w_ffn_loaded, 16)
            act.dma_start(bexp[:, :], b_exp.rearrange("(o n) -> o n", o=1)).then_inc(w_ffn_loaded, 16)
            act.dma_start(upb[:, :], up_b.rearrange("(o n) -> o n", o=1)).then_inc(w_ffn_loaded, 16)
            act.dma_start(bcon[:, :], b_con.partition_broadcast(P)).then_inc(w_ffn_loaded, 16)
            act.dma_start(bdown[:, :], down_b.partition_broadcast(P)).then_inc(w_ffn_loaded, 16)

            def copy_xt(b):
                for k in range(2):
                    act.wait_ge(xt_mm, 2 * b + k + 1)
                    nc.scalar.copy(xt[:, k * 512:(k + 1) * 512], ps[:, k, :]).then_inc(xt_ready, 1)

            act.wait_ge(setup_copied, 1)
            copy_xt(0)
            for b in range(B):
                for w in range(2):
                    act.wait_ge(qk_mm, 2 * b + w + 1)
                    nc.scalar.activation(qkf[:, w, :].rearrange("p (k n) -> p k n", k=2),
                                         ps[:, 2 + 2 * w:4 + 2 * w, :], ACT.Identity,
                                         bias=bqk[:, w:w + 1]).then_inc(qkf_ready, 1)
                act.wait_ge(qkf_ready, 2 * b + 2)
                if b > 1:
                    act.wait_ge(parts_stored[b % 2], 16 * STORES * (b // 2))
                nc.scalar.copy(qkp[:, b % 2, 0, :, :], qkf[:, :, :]).then_inc(part1_ready, 1)
                if b + 1 < B:
                    copy_xt(b + 1)
                act.wait_ge(res1_ready, b + 1)
                nc.scalar.copy(qkp[:, b % 2, 1, :, :], qkr[:, :, :]).then_inc(part2_ready, 1)
            act.wait_ge(setup_mm, 2)
            nc.scalar.copy(dn_y[:, 1, :], ps[:, 0, :]).then_inc(setup_copied, 1)

            def copy_o(turn, du):
                act.wait_ge(pv_done, turn * STEP_IT + STEPS * (du + 1))
                if du == 3:
                    act.wait_ge(o_stored[0], turn * (2 * OST) + 2 * OST)
                    act.wait_ge(o_stored[1], turn * (2 * OST) + OST)
                nc.scalar.copy(osb[:, du, :], ps[:, 6, :]).then_inc(o_bank_free, 1)

            def weights(turn):
                for s in range(STEP_IT):
                    if s % STEPS == 1 and s > 1:
                        copy_o(turn, s // STEPS - 1)
                    for j in range(2):
                        n = 2 * s + j
                        act.wait_ge(exp_scores, turn * 2 * STEP_IT + n + 1)
                        if j == 0 and s > 1:
                            act.wait_ge(pv_done, turn * STEP_IT + s - 1)
                        nc.scalar.activation(pr[:, n % 4, :, :], ps[:, 2 + 2 * j:4 + 2 * j, :],
                                             ACT.Exp).then_inc(exp_done, 1)
                copy_o(turn, 3)

            act.wait_ge(o_bank_free, 1)
            with act.Fori(0, TURNS - 1) as turn:
                weights(turn)
            weights(TURNS - 1)

            act.wait_ge(ffn_mm, 2)
            nc.scalar.copy(wdn[:, :, :], ps[:, 5, :]).then_inc(ffn_w_ready, 1)
            nc.scalar.copy(bup[:, :], ps[:, 6, 0:HC]).then_inc(ffn_w_ready, 1)
            act.wait_ge(ffn_w_ready, 2)

            def copy_att(t):
                act.wait_ge(att_tr, t + 1)
                nc.scalar.copy(att_t[:, :], ps[:, 2, :]).then_inc(att_t_ready, 1)

            def copy_x1(t, s):
                act.wait_ge(x1_tr, t + 1)
                nc.scalar.copy(x1t[:, s, :], ps[:, 4, :]).then_inc(x1t_ready, 1)

            def gelu(t, c):
                act.wait_ge(h_mm, t * HC + c + 1)
                nc.scalar.activation(gt[:, c, :], ps[:, 5 + c % 2, :], ACT.Gelu,
                                     bias=bup[:, c:c + 1]).then_inc(gelu_done, 1)

            def block_act(t, s, last):
                gelu(t, 0)
                gelu(t, 1)
                if not last:
                    copy_att(t + 1)
                gelu(t, 2)
                gelu(t, 3)
                if not last:
                    copy_x1(t + 1, 1 - s)

            copy_att(0)
            copy_x1(0, 0)
            with act.Fori(0, BLOCKS // 2 - 1) as i:
                for s in range(2):
                    block_act(i * 2 + s, s, False)
            block_act(BLOCKS - 2, 0, False)
            block_act(BLOCKS - 1, 1, True)

        @block.vector
        def _(dve):
            def batch_stats(b):
                dve.wait_ge(x_loaded[b], 16)
                for t in range(KT):
                    last = nc.vector.bn_stats(stats[:, t, :], x_all[:, b * KT + t, :])
                last.then_inc(stats_ready, 1)
                dve.wait_ge(stats_ready, b + 1)
                for t in range(KT):
                    last = nc.vector.bn_aggr(mv[:, b % 2, t, :], stats[:, t, :])
                last.then_inc(mv_ready, 1)

            def batch_xn(b):
                dve.wait_ge(rstd_ready, b + 1)
                dve.wait_ge(mv_ready, b + 1)
                for t in range(KT):
                    last = nc.vector.tensor_scalar(xn[:, t, :], x_all[:, b * KT + t, :], mv[:, b % 2, t, 0:1],
                                                   rstd[:, b % 2, t:t + 1], ALU.subtract, ALU.mult)
                last.then_inc(xn_ready, 1)

            batch_stats(0)
            dve.wait_ge(w_attn_loaded, 16 * N_ATTN_W)
            for w in range(2):
                nc.vector.tensor_copy(wqk[:, w, :].rearrange("p (g e h) -> p g e h", e=D, h=HG),
                                      wqkv[:, w * E:(w + 1) * E].rearrange("p (g h e) -> p g e h", e=D, h=HG)
                                      ).then_inc(perm_ready, 1)
                nc.vector.tensor_copy(brow_qk[:, w, :].rearrange("p (g e h) -> p g e h", e=D, h=HG),
                                      brow[:, w * E:(w + 1) * E].rearrange("p (g h e) -> p g e h", e=D, h=HG)
                                      ).then_inc(perm_ready, 1)
            batch_xn(0)
            dve.wait_ge(setup_mm, 1)
            nc.vector.tensor_copy(bqk[:, :], ps[:, 7, 0:2]).then_inc(setup_copied, 1)
            dve.wait_ge(vones_ready, 1)
            for b in range(B):
                s = b % 2
                if b + 1 < B:
                    batch_stats(b + 1)
                dve.wait_ge(v_mm, b + 1)
                if b > 1:
                    dve.wait_ge(parts_stored[s], 16 * STORES * (b // 2))
                for t in range(KT):
                    last = nc.vector.tensor_tensor(
                        vst[:, s, :, t, :, 0:D],
                        ps[:, 6 + t // 4, (t % 4) * P:(t % 4 + 1) * P].rearrange("p (g h e) -> p g h e", h=HG, e=D),
                        bv[:, :].rearrange("p (g h e) -> p g h e", h=HG, e=D), ALU.add)
                last.then_inc(v_copied, 1)
                if b + 1 < B:
                    batch_xn(b + 1)
                dve.wait_ge(part1_ready, b + 1)
                if b > 0:
                    dve.wait_ge(part2_ready, b)
                    dve.wait_ge(part3_ready, b)
                nc.vector.tensor_tensor(qkr[:, :, :], qkf[:, :, :], qkp[:, s, 0, :, :],
                                        ALU.subtract).then_inc(res1_ready, 1)

            dve.wait_ge(v_copied, B)
            nc.vector.memset(ps[:, 6, :], 0.0).then_inc(o_bank_free, 1)

            def split_maxima(turn, du, step):
                if step == 0:
                    dve.wait_ge(max_read, turn * TURN_FILLS + fill_of(du * STEPS + STEPS - 1, 3) + 1)
                    ins = nc.vector.tensor_reduce(negm[:, :], mx[:, du % 2, :, :], AX.X, ALU.max, negate=True)
                else:
                    dve.wait_ge(mchain, turn * (4 * CH) + du * CH + step)
                if step == 1:
                    ins = nc.vector.tensor_copy(mparts[:, 0:HG * QT], negm[:, :])
                if step == 2:
                    ins = nc.vector.tensor_tensor(mres[:, :], negm[:, :], mparts[:, 0:HG * QT], ALU.subtract)
                if step == 3:
                    ins = nc.vector.tensor_copy(mparts[:, HG * QT:2 * HG * QT], mres[:, :])
                if step == 4:
                    ins = nc.vector.tensor_tensor(mparts[:, 2 * HG * QT:3 * HG * QT], mres[:, :],
                                                  mparts[:, HG * QT:2 * HG * QT], ALU.subtract)
                ins.then_inc(mchain, 1)

            def copy_m(turn, du, last=False):
                n = fill_of_m(du, last)
                dve.wait_ge(max_scores, turn * TURN_FILLS + n + 1)
                nc.vector.tensor_copy(mrow[:, :], ps[:, ROT[n % 3], :].bitcast(BF16)[0:PARTS * HG * QT, 0:P]
                                      ).then_inc(max_read, 1)

            def maxima(turn, c):
                r, u = c % STEPS, c // STEPS
                for k in range(4):
                    n = fill_of(c, k)
                    dve.wait_ge(max_scores, turn * TURN_FILLS + n + 1)
                    col = (r // 2) * QT + (r % 2) * 2 + k // 2
                    nc.vector.tensor_reduce(mx[:, u % 2, col, k % 2:k % 2 + 1], ps[:, ROT[n % 3], :], AX.X,
                                            ALU.max).then_inc(max_read, 1)
                    if c >= STEPS and 4 * r + k < CH:
                        split_maxima(turn, u - 1, 4 * r + k)
                if r == 1 and c > 1:
                    copy_m(turn, u - 1)

            for c in range(LEAD):
                maxima(0, c)
            with dve.Fori(0, TURNS - 1) as turn:
                for s in range(STEP_IT):
                    maxima(turn, s + LEAD)
            for s in range(STEP_IT - LEAD):
                maxima(TURNS - 1, s + LEAD)
            for step in range(CH):
                split_maxima(TURNS - 1, 3, step)
            copy_m(TURNS - 1, 3, True)

            def chain(base):
                done = [base]

                def then(ins):
                    ins.then_inc(dch, 1)
                    done[0] = done[0] + 1
                    dve.wait_ge(dch, done[0])
                return then

            def normalise(y, dst, then, n):
                for t in range(BT):
                    last = nc.vector.bn_stats(st3[:, t, :], y[:, t, :])
                then(last)
                nc.vector.tensor_copy(carrier[:, :], st3[:, 0, 0:1])
                for t in range(BT):
                    last = nc.vector.bn_aggr(mv3[:, t, :], st3[:, t, :])
                last.then_inc(ln_mv, 1)
                dve.wait_ge(ln_mv, n + 1)
                dve.wait_ge(ln_rstd, n + 1)
                for t in range(BT):
                    last = nc.vector.tensor_scalar(dst[:, t, :], y[:, t, :], mv3[:, t, 0:1], rs3[:, t:t + 1],
                                                   ALU.subtract, ALU.mult)
                return last

            def front(t, s, base, n):
                then = chain(base)
                dve.wait_ge(o_tr, t + 1)
                o = ps[:, 0:2, 0:2 * H * VW].rearrange("p k (t c) -> p k t c", c=VW)
                r = rec[:, :].rearrange("p (k t) -> p k t", k=2)
                then(nc.vector.reciprocal(r, o[:, :, :, D]))
                nc.vector.tensor_tensor(att[:, :, :].rearrange("p (k t) (h d) -> p k (t h) d", k=2, d=D),
                                        o[:, :, :, 0:D], r.unsqueeze(3).to_broadcast([P, 2, 2 * H, D]),
                                        ALU.mult).then_inc(att_ready, 1)
                dve.wait_ge(y_mm, t + 1)
                then(nc.vector.tensor_tensor(yb[:, :, :], ps[:, 3, :].rearrange("p (t e) -> p t e", e=E),
                                             bout[:, :].unsqueeze(1).to_broadcast([P, BT, E]), ALU.add))
                then(normalise(yb, yb, then, n))
                then(nc.vector.tensor_tensor(x1[:, s, :, :], yb[:, :, :], x_all[:, bass.ds(t * BT, BT), :],
                                             ALU.add))
                normalise(x1[:, s], x1n, then, n + 1).then_inc(x1n_ready, 1)

            def back(t, s, base, n, last):
                then = chain(base)
                if last:
                    dve.wait_ge(res_ready, t)
                dve.wait_ge(y2_mm, t + 1)
                ins = nc.vector.tensor_tensor(y2[:, :, :], ps[:, 7, :].rearrange("p (t e) -> p t e", e=E),
                                              bffn[:, :].unsqueeze(1).to_broadcast([P, BT, E]), ALU.add)
                ins.then_inc(y2_read, 1)
                dve.wait_ge(y2_read, t + 1)
                then(normalise(y2, y2, then, n))
                nc.vector.tensor_tensor(x_all[:, bass.ds(t * BT, BT), :], y2[:, :, :], x1[:, s, :, :],
                                        ALU.add).then_inc(res_ready, 1)

            FRONT, BACK = 6, 2

            def block_dve(t, s, last):
                base = t * (FRONT + BACK) + FRONT
                if not last:
                    front(t + 1, 1 - s, base, t * 3 + 2)
                    back(t, s, base + FRONT, t * 3 + 4, False)
                else:
                    back(t, s, base, t * 3 + 2, True)

            dve.wait_ge(w_out_loaded, 32)
            front(0, 0, 0, 0)
            dve.wait_ge(bf_step, BF_STEPS)
            with dve.Fori(0, BLOCKS // 2 - 1) as i:
                for s in range(2):
                    block_dve(i * 2 + s, s, False)
            block_dve(BLOCKS - 2, 0, False)
            block_dve(BLOCKS - 1, 1, True)

        @block.tensor
        def _(pe):
            pe.wait_ge(perm_ready, 4)
            pe.wait_ge(consts_ready, 8)
            for w in range(2):
                last = nc.tensor.matmul(ps[:, 7, w:w + 1], brow_qk[0:1, w, :], one[:, :], start=True, stop=True)
            last.then_inc(setup_mm, 1)

            for b in range(B):
                pe.wait_ge(xn_ready, b + 1)
                for t in range(KT):
                    last = nc.tensor.transpose(ps[:, t // 4, (t % 4) * P:(t % 4 + 1) * P], xn[:, t, :], ident[:, :])
                    if t % 4 == 3:
                        last.then_inc(xt_mm, 1)
                pe.wait_ge(xt_ready, 2 * b + 2)
                if b > 0:
                    pe.wait_ge(qkf_ready, 2 * b)
                for w in range(2):
                    for k in range(2):
                        last = nc.tensor.matmul(ps[:, 2 + 2 * w + k, :], wqk[:, w, :], xt[:, k * 512:(k + 1) * 512],
                                                start=True, stop=True)
                    last.then_inc(qk_mm, 1)
                if b == 0:
                    pe.wait_ge(setup_copied, 1)
                else:
                    pe.wait_ge(v_copied, b)
                for t in range(KT):
                    last = nc.tensor.matmul(ps[:, 6 + t // 4, (t % 4) * P:(t % 4 + 1) * P],
                                            xt[:, t * P:(t + 1) * P], wqkv[:, 2 * E:3 * E], start=True, stop=True)
                last.then_inc(v_mm, 1)
            pe.wait_ge(w_ffn_loaded, 16 * N_FFN_W)
            for c in range(HC):
                last = nc.tensor.transpose(ps[:, 0, c * P:(c + 1) * P], wcon[:, c, :], ident[:, :])
            last.then_inc(setup_mm, 1)
            pe.wait_ge(setup_copied, 2)
            pe.wait_ge(qkf_ready, 2 * B)
            pe.wait_ge(v_copied, B)
            pe.wait_ge(o_bank_free, 1)

            def transpose_m(turn, du, last=False):
                n = fill_of_m(du, last)
                pe.wait_ge(mchain, turn * (4 * CH) + (du + 1) * CH)
                pe.wait_ge(max_read, turn * TURN_FILLS + n - 2)
                nc.tensor.transpose(ps[:, ROT[n % 3], :].bitcast(BF16)[0:MW, 0:P], mparts[:, :],
                                    ident_bf[:, :]).then_inc(max_scores, 1)

            def max_fill(turn, c, k):
                r, slot, j, half = c % STEPS, (c // (2 * STEPS)) % 2, k // 2, k % 2
                if c % (2 * STEPS) == 0 and k == 0:
                    pe.wait_ge(kq_loaded[slot], (turn + c // STEP_IT + 1) * KQ)
                h, qt, qhalf = r // 2, (r % 2) * 2 + j, (c // STEPS) % 2
                n = fill_of(c, k)
                if n > 2:
                    pe.wait_ge(max_read, turn * TURN_FILLS + n - 2)
                nc.tensor.matmul(ps[:, ROT[n % 3], :], qx[0:PROD, slot, qhalf, h, qt * P:(qt + 1) * P],
                                 kx[0:PROD, slot, h, half * 512:(half + 1) * 512],
                                 start=True, stop=True).then_inc(max_scores, 1)
                if r == 1 and k == 3 and c > 1:
                    transpose_m(turn, c // STEPS - 1)

            def score_pair(turn, s, j):
                slot, half, kt = s // (2 * STEPS), s // STEPS % 2, s % STEPS
                if kt == 0 and j == 0:
                    pe.wait_ge(m_rows_loaded, (turn * 4 + s // STEPS + 1) * MROW)
                if s > 0:
                    pe.wait_ge(exp_done, turn * (2 * STEP_IT) + 2 * s + j - 1)
                for h in range(2):
                    last = nc.tensor.matmul(ps[:, 2 + 2 * j + h, :], kx[0:ROWS, slot, 2 * j + h, kt * P:(kt + 1) * P],
                                            qx[0:ROWS, slot, half, 2 * j + h, :],
                                            start=True, stop=True)
                last.then_inc(exp_scores, 1)

            def weigh_v(turn, s):
                slot, kt = s // (2 * STEPS), s % STEPS
                pe.wait_ge(exp_done, turn * (2 * STEP_IT) + 2 * s + 2)
                if s % (2 * STEPS) == 0:
                    pe.wait_ge(v_loaded[slot], (turn + 1) * 16)
                if kt == 0:
                    pe.wait_ge(o_bank_free, turn * 4 + s // STEPS + 1)
                for h in range(HG):
                    last = nc.tensor.matmul(ps[32 * h:32 * h + VW, 6, :], vg[:, slot, kt, h, :],
                                            pr[:, 2 * (s % 2) + h // 2, h % 2, :],
                                            start=(kt == 0), stop=(kt == STEPS - 1))
                last.then_inc(pv_done, 1)

            def turn_pe(turn, last_turn):
                for s in range(STEP_IT):
                    ahead = not last_turn or s + LEAD < STEP_IT
                    end = s == STEP_IT - 1

                    def maxima(k):
                        if ahead:
                            max_fill(turn, s + LEAD, k)

                    if not end:
                        score_pair(turn, s, 0)
                        maxima(0)
                        score_pair(turn, s, 1)
                        maxima(1)
                        if s > 0:
                            weigh_v(turn, s - 1)
                        maxima(2)
                        maxima(3)
                    else:
                        score_pair(turn, s, 0)
                        maxima(0)
                        score_pair(turn, s, 1)
                        weigh_v(turn, s - 1)
                        maxima(1)
                        maxima(2)
                        maxima(3)
                        weigh_v(turn, s)
                    if last_turn and s + LEAD == STEP_IT:
                        transpose_m(turn, 3, True)

            for c in range(LEAD):
                for k in range(4):
                    max_fill(0, c, k)
            with pe.Fori(0, TURNS - 1) as turn:
                turn_pe(turn, False)
            turn_pe(TURNS - 1, True)

            pe.wait_ge(w_out_loaded, 32)
            pe.wait_ge(bf_step, BF_STEPS)
            pe.wait_ge(exp_done, 2 * STEP_IT * TURNS)
            pe.wait_ge(o_bank_free, UNITS + 1)
            pe.wait_ge(max_read, TURN_FILLS * TURNS)
            for c in range(HC):
                last = nc.tensor.transpose(ps[:, 5, c * P:(c + 1) * P], dn_y[:, 0, c * P:(c + 1) * P], ident[:, :])
            last.then_inc(ffn_mm, 1)
            for c in range(HC):
                last = nc.tensor.matmul(ps[:, 6, c:c + 1], row_y[0:1, 1, c * P:(c + 1) * P], one[:, :],
                                        start=True, stop=True)
            last.then_inc(ffn_mm, 1)

            def untranspose(t, s, use):
                pe.wait_ge(o_in_loaded[s], (use + 1) * 32)
                rows = 2 * HG * VW
                for tt in range(BT):
                    for j in range(2):
                        c = (tt % 2) * 2 * rows + j * rows
                        last = nc.tensor.transpose(ps[:, tt // 2, c:c + rows], o_in[:, s, j, tt * P:(tt + 1) * P],
                                                   ident[0:rows, 0:rows])
                last.then_inc(o_tr, 1)

            def transpose_att(t):
                pe.wait_ge(att_ready, t + 1)
                for tt in range(BT):
                    last = nc.tensor.transpose(ps[:, 2, tt * P:(tt + 1) * P], att[:, tt, :], ident[:, :])
                last.then_inc(att_tr, 1)

            def project_out(t):
                pe.wait_ge(att_t_ready, t + 1)
                for tt in range(BT):
                    last = nc.tensor.matmul(ps[:, 3, tt * P:(tt + 1) * P], att_t[:, tt * P:(tt + 1) * P], wout[:, :],
                                            start=True, stop=True)
                last.then_inc(y_mm, 1)

            def transpose_x1(t):
                pe.wait_ge(x1n_ready, t + 1)
                for tt in range(BT):
                    last = nc.tensor.transpose(ps[:, 4, tt * P:(tt + 1) * P], x1n[:, tt, :], ident[:, :])
                last.then_inc(x1_tr, 1)

            def hidden(t, s, c):
                if c == 0:
                    pe.wait_ge(x1t_ready, t + 1)
                if c > 1:
                    pe.wait_ge(gelu_done, t * HC + c - 1)
                nc.tensor.matmul(ps[:, 5 + c % 2, :], up_y[:, 0, c * P:(c + 1) * P], x1t[:, s, :],
                                 start=True, stop=True).then_inc(h_mm, 1)

            def contract(t, last):
                pe.wait_ge(gelu_done, t * HC + HC)
                if last:
                    pe.wait_ge(y2_read, t)
                for tt in range(BT):
                    for c in range(HC):
                        last = nc.tensor.matmul(ps[:, 7, tt * P:(tt + 1) * P], gt[:, c, tt * P:(tt + 1) * P],
                                                wdn[:, c, :], start=(c == 0), stop=(c == HC - 1))
                last.then_inc(y2_mm, 1)

            def block_pe(t, s, last, use):
                if not last:
                    untranspose(t + 1, 1 - s, use)
                hidden(t, s, 0)
                hidden(t, s, 1)
                if not last:
                    transpose_att(t + 1)
                hidden(t, s, 2)
                hidden(t, s, 3)
                if not last:
                    project_out(t + 1)
                contract(t, last)
                if not last:
                    transpose_x1(t + 1)

            untranspose(0, 0, 0)
            transpose_att(0)
            project_out(0)
            transpose_x1(0)
            pe.wait_ge(ffn_w_ready, 2)
            with pe.Fori(0, BLOCKS // 2 - 1) as i:
                block_pe(i * 2, 0, False, i)
                block_pe(i * 2 + 1, 1, False, i + 1)
            block_pe(BLOCKS - 2, 0, False, BLOCKS // 2 - 1)
            block_pe(BLOCKS - 1, 1, True, 0)

    return nc


NAMES = ["L0_attn_x", "L0_attn_W_qkv", "L0_attn_b_qkv", "L0_attn_W_out", "L0_attn_b_out", "L0_ffn_W_exp",
         "L0_ffn_b_exp", "L0_ffn_up_weights", "L0_ffn_up_bias", "L0_ffn_down_weights", "L0_ffn_W_con",
         "L0_ffn_b_con", "L0_ffn_down_bias"]


def kernel(**inputs):
    import concourse.bacc as bacc
    from concourse.bass_utils import run_bass_kernel_spmd

    nc = bacc.Bacc("TRN2", target_bir_lowering=False, num_devices=1)
    arrays, args = {}, []
    for name in NAMES:
        a = np.ascontiguousarray(inputs[name])
        arrays[name] = a
        args.append(nc.dram_tensor(name, a.shape, mybir.dt.from_np(a.dtype), kind="ExternalInput").ap())
    out = nc.dram_tensor("out", (B, N, E), FP32, kind="ExternalOutput").ap()
    attention_ffn_kernel(nc, *args, out)
    got = run_bass_kernel_spmd(nc, [arrays], core_ids=[0])
    return got.results[0]["out"]
```

```python
import math
from contextlib import ExitStack

import numpy as np

import concourse.bass as bass
from concourse import mybir

FP32 = mybir.dt.float32
BF16 = mybir.dt.bfloat16
ALU = mybir.AluOpType
ACT = mybir.ActivationFunctionType
AX = mybir.AxisListType

P = 128
B, N, E = 4, 1024, 128
H = 16
D = E // H
HG = 4
NG = H // HG
GROUPS = B * NG
KT = N // P
TILES = B * KT
QH = N // 2
QT = QH // P
UNITS = GROUPS * 2
PARTS = 3
PROD = PARTS * PARTS * D
ROWS = PROD + PARTS
VW = D + 1
HID = 512
HC = HID // P
STAGES = int(math.log2(HID))
EPS = 1e-5
ONES_BF16 = float(np.array([0x3F803F80], np.uint32).view(np.float32)[0])
ROT = (0, 1, 7)
MW = 96
LEAD = 12
STEPS = KT
TB = 512
BT = TB // P
BLOCKS = B * N // TB


def attention_ffn_kernel(nc, x, w_qkv, b_qkv, w_out, b_out, w_exp, b_exp, up_w, up_b, down_w,
                         w_con, b_con, down_b, out):
    q_dram = nc.dram_tensor("q_parts", (GROUPS, PARTS, D * HG, N), BF16, kind="Internal").ap()
    k_dram = nc.dram_tensor("k_parts", (GROUPS, PARTS, D * HG, N), BF16, kind="Internal").ap()
    v_dram = nc.dram_tensor("v_ones", (GROUPS, P, KT * HG * VW), FP32, kind="Internal").ap()
    o_dram = nc.dram_tensor("o_sums", (GROUPS, 2, HG * VW, QH), FP32, kind="Internal").ap()

    ctx = ExitStack()
    with ctx:
        def sb(name, shape, dt=FP32):
            return ctx.enter_context(nc.sbuf_tensor(name, shape, dt))

        def sem(name):
            return ctx.enter_context(nc.semaphore(name))

        wqkv = sb("wqkv", [P, 3 * E])
        wqk = sb("wqk", [P, 2, E])
        brow = sb("brow", [1, 3 * E])
        brow_qk = sb("brow_qk", [1, 2, E])
        bqk = sb("bqk", [P, 2])
        bv = sb("bv", [P, E])
        wout = sb("wout", [P, E])
        bout = sb("bout", [P, E])
        wexp = sb("wexp", [P, HID])
        wcon = sb("wcon", [P, HC, E])
        bexp = sb("bexp", [1, HID])
        upb = sb("upb", [1, HID])
        bcon = sb("bcon", [P, E])
        bdown = sb("bdown", [P, E])
        bffn = sb("bffn", [P, E])
        ident = sb("ident", [P, P])
        ident_bf = sb("ident_bf", [P, P], BF16)
        one = sb("one", [1, 1])
        neghalf = sb("neghalf", [P, KT])
        eps_c = sb("eps_c", [P, KT])
        carrier = sb("carrier", [P, 1])
        first_use = sb("first_use", [1, 1])

        wst = sb("wst", [P, 2, 4 * HID // 2])
        up_y = sb("up_y", [P, 2, HID])
        dn_y = sb("dn_y", [P, 2, HID])
        row_y = sb("row_y", [1, 2, HID])
        bf_t = sb("bf_t", [P, 2, HID])
        wdn = sb("wdn", [P, HC, E])
        bup = sb("bup", [P, HC])

        x_all = sb("x_all", [P, TILES, E])
        stats = sb("stats", [P, KT, 6])
        mv = sb("mv", [P, 2, KT, 2])
        veps = sb("veps", [P, KT])
        rstd = sb("rstd", [P, 2, KT])

        qx = sb("qx", [P, 2, 2, HG, QH], BF16)
        kx = sb("kx", [P, 2, HG, N], BF16)
        vg = sb("vg", [P, 2, KT, HG, VW])
        pr = sb("pr", [P, 4, 2, QH])
        mx = sb("mx", [P, 2, HG * QT, 2])
        negm = sb("negm", [P, HG * QT])
        mres = sb("mres", [P, HG * QT])
        mparts = sb("mparts", [P, MW], BF16)
        mrow = sb("mrow", [PARTS * HG * QT, P], BF16)

        xn = sb("xn", [P, KT, E])
        xt = sb("xt", [P, 2, N])
        qkf = sb("qkf", [P, 2, N])
        qkr = sb("qkr", [P, 2, N])
        osb = qkr[:, :, :].rearrange("p w (c t) -> p (w c) t", t=QH)
        qkp = sb("qkp", [P, 2, PARTS, 2, N], BF16)
        vst = sb("vst", [P, 2, NG, KT, HG, VW])

        o_in = sb("o_in", [2 * HG * VW, 2, 2, TB])
        rec = sb("rec", [P, BT * H])
        att = xn[:, 0:BT, :]
        att_t = xt[:, 0, 0:TB]
        yb = xn[:, BT:2 * BT, :]
        y2 = sb("y2", [P, BT, E])
        y2n = sb("y2n", [P, BT, E])
        x1n = sb("x1n", [P, BT, E])
        x1t = sb("x1t", [P, TB])
        st3 = sb("st3", [P, 3, BT, 6])
        mv3 = sb("mv3", [P, 3, BT, 2])
        ve3 = sb("ve3", [P, 3, BT])
        nm3 = sb("nm3", [P, 3, BT])
        rs3 = sb("rs3", [P, 3, BT])
        nb3 = sb("nb3", [P, 3, BT])
        zeros = sb("zeros", [P, 2, BT])
        gt = qkf[:, :, :].rearrange("p w (c t) -> p (w c) t", t=TB)

        ps = ctx.enter_context(nc.psum_tensor("ps", [P, 8, 512], FP32))

        w_attn_loaded = sem("w_attn_loaded")
        w_ffn_loaded = sem("w_ffn_loaded")
        w_out_loaded = sem("w_out_loaded")
        x_loaded = [sem(f"x_loaded{b}") for b in range(B)]
        consts_ready = sem("consts_ready")
        ones_cleared = sem("ones_cleared")
        perm_ready = sem("perm_ready")
        setup_mm = sem("setup_mm")
        setup_copied = sem("setup_copied")
        stats_ready = sem("stats_ready")
        mv_ready = sem("mv_ready")
        veps_ready = sem("veps_ready")
        rstd_ready = sem("rstd_ready")
        xn_ready = sem("xn_ready")
        xt_mm = sem("xt_mm")
        xt_ready = sem("xt_ready")
        qk_mm = sem("qk_mm")
        v_mm = sem("v_mm")
        qkf_ready = sem("qkf_ready")
        v_copied = sem("v_copied")
        part1_ready = sem("part1_ready")
        res1_ready = sem("res1_ready")
        part2_ready = sem("part2_ready")
        part3_ready = sem("part3_ready")
        parts_stored = [sem(f"parts_stored{s}") for s in range(2)]
        kq_loaded = [sem(f"kq_loaded{s}") for s in range(2)]
        v_loaded = [sem(f"v_loaded{s}") for s in range(2)]
        max_scores = sem("max_scores")
        max_read = sem("max_read")
        mchain = sem("mchain")
        m_rows_loaded = sem("m_rows_loaded")
        exp_scores = sem("exp_scores")
        exp_done = sem("exp_done")
        pv_done = sem("pv_done")
        o_bank_free = sem("o_bank_free")
        o_stored = [sem(f"o_stored{s}") for s in range(2)]
        bf_loaded = [sem(f"bf_loaded{s}") for s in range(2)]
        bf_step = sem("bf_step")
        ffn_mm = sem("ffn_mm")
        ffn_w_ready = sem("ffn_w_ready")
        o_in_loaded = [sem(f"o_in_loaded{s}") for s in range(2)]
        o_tr = sem("o_tr")
        rec_ready = sem("rec_ready")
        att_ready = sem("att_ready")
        att_tr = sem("att_tr")
        att_t_ready = sem("att_t_ready")
        y_mm = sem("y_mm")
        y_read = sem("y_read")
        st_ready = sem("st_ready")
        mv_pair = sem("mv_pair")
        pool_pair = sem("pool_pair")
        rs_pair = sem("rs_pair")
        y_normed = sem("y_normed")
        x1_ready = sem("x1_ready")
        x1n_ready = sem("x1n_ready")
        x1_tr = sem("x1_tr")
        x1t_ready = sem("x1t_ready")
        h_mm = sem("h_mm")
        gelu_done = sem("gelu_done")
        y2_mm = sem("y2_mm")
        y2_read = sem("y2_read")
        st_out = sem("st_out")
        mv_out = sem("mv_out")
        pool_out = sem("pool_out")
        rs_out = sem("rs_out")
        y2_normed = sem("y2_normed")
        res_ready = sem("res_ready")
        vones_ready = sem("vones_ready")
        lnc_ready = sem("lnc_ready")
        res_stored = [sem(f"res_stored{s}") for s in range(2)]

        block = ctx.enter_context(nc.Block())

        N_ATTN_W, N_FFN_W = 3, 6
        STORES = 2 * PARTS + 1
        KQ = 16 * 3 * PARTS
        MROW = 16
        OST = 16 * HG
        CH = 5
        STEP_IT = 4 * STEPS
        TURNS = UNITS * STEPS // STEP_IT
        TURN_FILLS = 4 * (4 * STEPS + 1)
        assert TURN_FILLS % len(ROT) == 0
        BF_STEPS = 3 * 3 * STAGES + 2

        PIECES = [(0, 0, TB, 2), (1, 0, TB, 3), (2, 0, TB, 4), (3, 0, TB // 2, 6), (3, TB // 2, TB // 2, 2)]

        def fill_of(c, k):
            return 4 * c + k + (max(c - 2, 0) // STEPS)

        def fill_of_m(u, last=False):
            return fill_of(u * STEPS + STEPS - 1, 3) + 1 + (0 if last else 8)

        @block.sync
        def _(sp):
            for b in range(B):
                sp.dma_start(x_all[:, b * KT:(b + 1) * KT, :],
                             x[b].rearrange("(t p) e -> p t e", p=P)).then_inc(x_loaded[b], 16)
                if b == 0:
                    sp.dma_start(wqkv[:, :], w_qkv).then_inc(w_attn_loaded, 16)
                    sp.dma_start(brow[:, :], b_qkv.rearrange("(o n) -> o n", o=1)).then_inc(w_attn_loaded, 16)
                    sp.dma_start(bv[:, :], b_qkv[2 * E:].partition_broadcast(P)).then_inc(w_attn_loaded, 16)
            sp.dma_start(wout[:, :], w_out).then_inc(w_out_loaded, 16)
            sp.dma_start(bout[:, :], b_out.partition_broadcast(P)).then_inc(w_out_loaded, 16)

            def load_group(slot, group):
                for j in range(PARTS):
                    r = j * PARTS * D
                    for half in range(2):
                        sp.dma_start(qx[r:r + PARTS * D, slot, half, :, :],
                                     q_dram[bass.ds(group, 1), :, :, half * QH:(half + 1) * QH]
                                     .rearrange("o i (e h) t -> (o i e) h t", h=HG)).then_inc(kq_loaded[slot], 16)
                    sp.dma_start(kx[r:r + PARTS * D, slot].rearrange("r h t -> r (h t)"),
                                 k_dram[bass.ds(group, 1), j].rearrange("o (e h) t -> o e (h t)", h=HG)
                                 .to_broadcast([PARTS, D, HG * N])).then_inc(kq_loaded[slot], 16)

            def load_v(slot, group):
                sp.dma_start(vg[:, slot].rearrange("p t h c -> p (t h c)"),
                             v_dram[bass.ds(group, 1)].rearrange("o p f -> (o p) f")).then_inc(v_loaded[slot], 16)

            def load_m_rows(turn, du, last=False):
                sp.wait_ge(max_read, turn * TURN_FILLS + fill_of_m(du, last) + 1)
                slot, half = (du // 2) % 2, du % 2
                sp.dma_start(qx[PROD:ROWS, slot, half, :, :].rearrange("i h t -> i (h t)"),
                             mrow[:, :]).then_inc(m_rows_loaded, 16)

            def store_o(turn, du):
                half = du % 2
                sp.wait_ge(o_bank_free, turn * 4 + du + 2)
                for h in range(HG):
                    sp.dma_start(o_dram[bass.ds(turn * 2 + du // 2, 1), half, h * VW:(h + 1) * VW, :]
                                 .rearrange("o c t -> (o c) t"),
                                 osb[32 * h:32 * h + VW, du, :]).then_inc(o_stored[half], 16)

            def load_o(bt, half):
                for j in range(2):
                    sp.dma_start(o_in[:, half, j, :],
                                 o_dram[bass.ds(bt * NG + 2 * j, 2), half, :, :]).then_inc(o_in_loaded[half], 16)

            def store_res(bt, half):
                sp.wait_ge(res_ready, bt * 2 + half + 1)
                sp.dma_start(out[bass.ds(bt, 1), half * TB:(half + 1) * TB, :]
                             .rearrange("o (t p) e -> p (o t) e", p=P),
                             x_all[:, bass.ds((bt * 2 + half) * BT, BT), :]
                             ).then_inc(res_stored[half], 16)

            def turn_dmas(turn, last):
                load_m_rows(turn, 1)
                store_o(turn, 0)
                load_m_rows(turn, 2)
                if not last:
                    sp.wait_ge(exp_scores, turn * 2 * STEP_IT + STEP_IT)
                    load_group(0, turn * 2 + 2)
                store_o(turn, 1)
                if not last:
                    sp.wait_ge(pv_done, turn * STEP_IT + STEP_IT // 2)
                    load_v(0, turn * 2 + 2)
                load_m_rows(turn, 3, last)
                if last:
                    for t in (2, 3):
                        sp.wait_ge(o_tr, t - 1)
                        load_o(t // 2, t % 2)
                store_o(turn, 2)
                if not last:
                    load_m_rows(turn, 4)
                    sp.wait_ge(exp_scores, turn * 2 * STEP_IT + 2 * STEP_IT)
                    load_group(1, turn * 2 + 3)
                store_o(turn, 3)
                if not last:
                    sp.wait_ge(pv_done, turn * STEP_IT + STEP_IT)
                    load_v(1, turn * 2 + 3)

            def store_parts(b):
                s = b % 2
                for i, ready in enumerate((part1_ready, part2_ready, part3_ready)):
                    for w, dst in ((0, q_dram), (1, k_dram)):
                        sp.wait_ge(ready, 2 * b + w + 1)
                        sp.dma_start(dst[b * NG:(b + 1) * NG, i, :, :], qkp[:, s, i, w, :]
                                     ).then_inc(parts_stored[s], 16)
                    if i == 0:
                        sp.wait_ge(v_copied, b + 1)
                        sp.dma_start(v_dram[b * NG:(b + 1) * NG, :, :].rearrange("g p f -> p g f"),
                                     vst[:, s].rearrange("p g t h c -> p g (t h c)")).then_inc(parts_stored[s], 16)

            store_parts(0)
            store_parts(1)
            sp.wait_ge(ones_cleared, 2)
            sp.wait_ge(parts_stored[0], 16 * STORES)
            load_group(0, 0)
            load_v(0, 0)
            store_parts(2)
            store_parts(3)
            load_group(1, 1)
            load_v(1, 1)
            for s in range(2):
                sp.wait_ge(parts_stored[s], 16 * STORES * (B // 2))
            load_m_rows(0, 0)
            with sp.Fori(0, TURNS - 1) as turn:
                turn_dmas(turn, False)
            for half in range(2):
                sp.wait_ge(o_stored[half], OST * 3 * NG)
                load_o(0, half)
            turn_dmas(TURNS - 1, True)

            for t in (4, 5):
                sp.wait_ge(o_tr, t - 1)
                load_o(t // 2, t % 2)
            for half in range(2):
                sp.wait_ge(o_stored[half], OST * GROUPS)
            for t in (6, 7):
                sp.wait_ge(o_tr, t - 1)
                load_o(t // 2, t % 2)
                store_res(0, t % 2)
            with sp.Fori(1, B) as bt:
                for half in range(2):
                    store_res(bt, half)
            for half in range(2):
                sp.wait_ge(res_stored[half], 16 * B)

        @block.gpsimd
        def _(pool):
            nc.gpsimd.memset(ident[:, :], 0.0).then_inc(consts_ready, 1)
            nc.gpsimd.memset(ident_bf[:, :], 0.0).then_inc(consts_ready, 1)
            nc.gpsimd.memset(one[:, :], 1.0).then_inc(consts_ready, 1)
            nc.gpsimd.memset(neghalf[:, :], -0.5).then_inc(consts_ready, 1)
            nc.gpsimd.memset(eps_c[:, :], EPS).then_inc(consts_ready, 1)
            nc.gpsimd.memset(mparts[:, PARTS * HG * QT:], 0.0).then_inc(consts_ready, 1)
            pool.wait_ge(consts_ready, 6)
            nc.gpsimd.memset(mv3[:, :, :, :].rearrange("p n t c -> p (n t c)"), 1.0).then_inc(lnc_ready, 1)
            nc.gpsimd.memset(zeros[:, :, :], 0.0).then_inc(lnc_ready, 1)
            for m in (ident, ident_bf):
                nc.gpsimd.affine_select(out=m[:, :], in_=m[:, :], compare_op=ALU.not_equal, fill=1.0,
                                        base=0, pattern=[[-1, P]], channel_multiplier=1).then_inc(consts_ready, 1)

            def batch_rstd(b):
                pool.wait_ge(mv_ready, b + 1)
                nc.gpsimd.tensor_tensor(veps[:, :], mv[:, b % 2, :, 1], eps_c[:, :], ALU.add).then_inc(veps_ready, 1)
                pool.wait_ge(veps_ready, b + 1)
                if b > 1:
                    pool.wait_ge(xn_ready, b - 1)
                nc.gpsimd.tensor_tensor(rstd[:, b % 2, :], veps[:, :], neghalf[:, :], ALU.pow).then_inc(rstd_ready, 1)

            batch_rstd(0)
            nc.gpsimd.memset(vst[:, :, :, :, :, :].rearrange("p s g t h c -> p (s g t h c)"),
                             math.sqrt(E)).then_inc(vones_ready, 1)
            pool.wait_ge(vones_ready, 1)
            batch_rstd(1)
            pool.wait_ge(rstd_ready, 2)
            for slot in range(2):
                nc.gpsimd.memset(kx[64:96, slot, :, :].rearrange("p h t -> p (h t)").bitcast(FP32), ONES_BF16
                                 ).then_inc(ones_cleared, 1)
                pool.wait_ge(ones_cleared, slot + 1)
                batch_rstd(2 + slot)
                pool.wait_ge(rstd_ready, 3 + slot)

            for b in range(B):
                for w in range(2):
                    pool.wait_ge(part2_ready, 2 * b + w + 1)
                    if b > 0 or w > 0:
                        pool.wait_ge(part3_ready, 2 * b + w)
                    nc.gpsimd.tensor_tensor(qkp[:, b % 2, 2, w, :], qkr[:, w, :], qkp[:, b % 2, 1, w, :],
                                            ALU.subtract).then_inc(part3_ready, 1)

            steps = [0]

            def then(ins):
                ins.then_inc(bf_step, 1)
                steps[0] += 1
                pool.wait_ge(bf_step, steps[0])

            def butterfly(y_in, y_out, w, stride, rows, transposed):
                nb = HID // (2 * stride)
                y = y_in.rearrange("p (n r j) -> p n r j", r=2, j=stride)
                wv = w.rearrange("p (n j c) -> p n c j", j=stride, c=4)
                shape = [rows, nb, 2, stride]
                for r in range(2):
                    c = slice(2 * r, 2 * r + 2) if transposed else slice(r, r + 3, 2)
                    then(nc.gpsimd.tensor_tensor(
                        bf_t[0:rows, r, :].rearrange("p (n o j) -> p n o j", o=2, j=stride),
                        y[:, :, r:r + 1, :].to_broadcast(shape), wv[:, :, c, :], ALU.mult))
                then(nc.gpsimd.tensor_tensor(y_out, bf_t[0:rows, 0, :], bf_t[0:rows, 1, :], ALU.add))

            def load_stage(n):
                w, stage = (up_w, n) if n < STAGES else (down_w, 2 * STAGES - 1 - n)
                pool.dma_start(wst[:, n % 2, :],
                               w[stage].rearrange("k o i -> (k o i)").partition_broadcast(P)
                               ).then_inc(bf_loaded[n % 2], 16)

            load_stage(0)
            load_stage(1)
            pool.wait_ge(w_ffn_loaded, 16 * N_FFN_W)
            pool.wait_ge(setup_copied, 2)
            for n in range(2 * STAGES):
                pool.wait_ge(bf_loaded[n % 2], 16 * (n // 2 + 1))
                w = wst[:, n % 2, :]
                k = n % STAGES
                if n < STAGES:
                    butterfly(wexp[:, :] if k == 0 else up_y[:, (k + 1) % 2, :], up_y[:, k % 2, :], w,
                              2 ** k, P, False)
                    butterfly(bexp[:, :] if k == 0 else row_y[:, (k + 1) % 2, :], row_y[:, k % 2, :], w[0:1, :],
                              2 ** k, 1, False)
                else:
                    butterfly(dn_y[:, (k + 1) % 2, :], dn_y[:, k % 2, :], w, 2 ** (STAGES - 1 - k), P, True)
                if n + 2 < 2 * STAGES:
                    load_stage(n + 2)
            then(nc.gpsimd.tensor_tensor(row_y[:, 1, :], row_y[:, 0, :], upb[:, :], ALU.add))
            then(nc.gpsimd.tensor_tensor(bffn[:, :], bcon[:, :], bdown[:, :], ALU.add))
            assert steps[0] == BF_STEPS

            pool.wait_ge(lnc_ready, 2)

            def scales(norms, n, ready, local, done, used, value):
                rows = len(range(*norms.indices(3)))
                pool.wait_ge(ready, n + 1)
                nc.gpsimd.tensor_tensor(ve3[:, norms, :], mv3[:, norms, :, 1],
                                        eps_c[:, 0:rows * BT].rearrange("p (r t) -> p r t", t=BT),
                                        ALU.add).then_inc(local, 1)
                nc.gpsimd.tensor_tensor(nm3[:, norms, :], zeros[:, 0:rows, :], mv3[:, norms, :, 0],
                                        ALU.subtract).then_inc(local, 1)
                pool.wait_ge(local, n * 3 + 2)
                if used is not None:
                    pool.wait_ge(used, value)
                nc.gpsimd.tensor_tensor(rs3[:, norms, :], ve3[:, norms, :],
                                        neghalf[:, 0:rows * BT].rearrange("p (r t) -> p r t", t=BT),
                                        ALU.pow).then_inc(local, 1)
                pool.wait_ge(local, n * 3 + 3)
                nc.gpsimd.tensor_tensor(nb3[:, norms, :], nm3[:, norms, :], rs3[:, norms, :],
                                        ALU.mult).then_inc(done, 1)

            def add_x(t, y, ready, done):
                pool.wait_ge(ready, t + 1)
                nc.gpsimd.tensor_tensor(x_all[:, bass.ds(t * BT, BT), :], x_all[:, bass.ds(t * BT, BT), :], y,
                                        ALU.add).then_inc(done, 1)

            def turn_pool(k, front, pair, back, first=False, last=False):
                if pair:
                    scales(slice(0, 2), k + 2, mv_pair, pool_pair, rs_pair, None if first else x1n_ready,
                           None if first else k + 1)
                if back:
                    scales(slice(2, 3), k - 1, mv_out, pool_out, rs_out, None, 0)
                if front:
                    add_x(k + 2, yb[:, :, :], y_normed, x1_ready)
                if back:
                    if not last:
                        add_x(k - 1, y2n[:, :, :], y2_normed, res_ready)

            turn_pool(-2, True, True, False, first=True)
            turn_pool(-1, True, True, False, first=True)
            turn_pool(0, True, True, False)
            with pool.Fori(1, BLOCKS - 2) as k:
                turn_pool(k, True, True, True)
            turn_pool(BLOCKS - 2, False, True, True)
            turn_pool(BLOCKS - 1, False, False, True)
            turn_pool(BLOCKS, False, False, True, last=True)

        @block.scalar
        def _(act):
            act.dma_start(wexp[:, :], w_exp).then_inc(w_ffn_loaded, 16)
            act.dma_start(wcon[:, :, :], w_con.rearrange("(c p) e -> p c e", p=P)).then_inc(w_ffn_loaded, 16)
            act.dma_start(bexp[:, :], b_exp.rearrange("(o n) -> o n", o=1)).then_inc(w_ffn_loaded, 16)
            act.dma_start(upb[:, :], up_b.rearrange("(o n) -> o n", o=1)).then_inc(w_ffn_loaded, 16)
            act.dma_start(bcon[:, :], b_con.partition_broadcast(P)).then_inc(w_ffn_loaded, 16)
            act.dma_start(bdown[:, :], down_b.partition_broadcast(P)).then_inc(w_ffn_loaded, 16)

            act.wait_ge(consts_ready, 8)
            nc.scalar.copy(first_use[:, :], one[:, :])

            def copy_xt(b):
                for k in range(2):
                    act.wait_ge(xt_mm, 2 * b + k + 1)
                    nc.scalar.copy(xt[:, b % 2, k * 512:(k + 1) * 512], ps[:, k, :]).then_inc(xt_ready, 1)

            def add_bias(b, w):
                act.wait_ge(qk_mm, 2 * b + w + 1)
                if b > 0:
                    act.wait_ge(res1_ready, 2 * b + w - 1)
                nc.scalar.activation(qkf[:, w, :].rearrange("p (k n) -> p k n", k=2),
                                     ps[:, 2 + 2 * w:4 + 2 * w, :], ACT.Identity,
                                     bias=bqk[:, w:w + 1]).then_inc(qkf_ready, 1)

            def part1(b, w):
                act.wait_ge(qkf_ready, 2 * b + w + 1)
                if b > 1:
                    act.wait_ge(parts_stored[b % 2], 16 * STORES * (b // 2))
                nc.scalar.copy(qkp[:, b % 2, 0, w, :], qkf[:, w, :]).then_inc(part1_ready, 1)

            def part2(b, w):
                act.wait_ge(res1_ready, 2 * b + w + 1)
                nc.scalar.copy(qkp[:, b % 2, 1, w, :], qkr[:, w, :]).then_inc(part2_ready, 1)

            copy_xt(0)
            act.wait_ge(setup_copied, 1)
            for b in range(B):
                add_bias(b, 0)
                part1(b, 0)
                add_bias(b, 1)
                if b + 1 < B:
                    copy_xt(b + 1)
                part1(b, 1)
                part2(b, 0)
                part2(b, 1)
            act.wait_ge(setup_mm, 2)
            nc.scalar.copy(dn_y[:, 1, :], ps[:, 0, :]).then_inc(setup_copied, 1)

            def copy_o(turn, du):
                act.wait_ge(pv_done, turn * STEP_IT + STEPS * (du + 1))
                if du == 3:
                    act.wait_ge(o_stored[0], turn * (2 * OST) + 2 * OST)
                    act.wait_ge(o_stored[1], turn * (2 * OST) + OST)
                nc.scalar.copy(osb[:, du, :], ps[:, 6, :]).then_inc(o_bank_free, 1)

            def weights(turn, last_turn=False):
                for s in range(STEP_IT):
                    if s % STEPS == 1 and s > 1:
                        copy_o(turn, s // STEPS - 1)
                    for j in range(2):
                        n = 2 * s + j
                        act.wait_ge(exp_scores, turn * 2 * STEP_IT + n + 1)
                        if j == 0 and s > 1:
                            act.wait_ge(pv_done, turn * STEP_IT + s - 1)
                        nc.scalar.activation(pr[:, n % 4, :, :], ps[:, 2 + 2 * j:4 + 2 * j, :],
                                             ACT.Exp).then_inc(exp_done, 1)
                if last_turn:
                    nc.scalar.activation(first_use[:, :], one[:, :], ACT.Gelu)
                copy_o(turn, 3)

            act.wait_ge(o_bank_free, 1)
            with act.Fori(0, TURNS - 1) as turn:
                weights(turn)
            weights(TURNS - 1, True)

            act.wait_ge(ffn_w_ready, 2)

            def copy_x1(t):
                act.wait_ge(x1_tr, t + 1)
                nc.scalar.copy(x1t[:, :], ps[:, 7, :]).then_inc(x1t_ready, 1)

            def gelu(t, i):
                c, start, n, bank = PIECES[i]
                act.wait_ge(h_mm, t * len(PIECES) + i + 1)
                nc.scalar.activation(gt[:, c, start:start + n], ps[:, bank, start:start + n], ACT.Gelu,
                                     bias=bup[:, c:c + 1]).then_inc(gelu_done, 1)

            def copy_att(t):
                act.wait_ge(att_tr, t + 1)
                nc.scalar.copy(att_t[:, :], ps[:, 7, :]).then_inc(att_t_ready, 1)

            def norm0(k):
                act.wait_ge(rs_pair, k + 3)
                for tt in range(BT):
                    last = nc.scalar.activation(x1n[:, tt, :], x_all[:, bass.ds((k + 1) * BT + tt, 1), :]
                                                .rearrange("p o e -> p (o e)"), ACT.Identity,
                                                bias=nb3[:, 0, tt:tt + 1], scale=rs3[:, 0, tt:tt + 1])
                last.then_inc(x1n_ready, 1)

            def norm2(t):
                act.wait_ge(rs_out, t + 1)
                for tt in range(BT):
                    last = nc.scalar.activation(y2n[:, tt, :], y2[:, tt, :], ACT.Identity,
                                                bias=nb3[:, 2, tt:tt + 1], scale=rs3[:, 2, tt:tt + 1])
                last.then_inc(y2_normed, 1)

            def turn_act(k, front, mid, ffn, back):
                if ffn:
                    for i in range(len(PIECES)):
                        gelu(k, i)
                if front:
                    copy_att(k + 3)
                if mid:
                    norm0(k)
                    copy_x1(k + 1)
                if back:
                    norm2(k - 1)

            turn_act(0, True, True, True, False)
            with act.Fori(1, BLOCKS - 3) as k:
                turn_act(k, True, True, True, True)
            for k in range(BLOCKS - 3, BLOCKS):
                turn_act(k, False, k + 1 < BLOCKS, k < BLOCKS, True)

        @block.vector
        def _(dve):
            def batch_stats(b):
                dve.wait_ge(x_loaded[b], 16)
                if b > 0:
                    dve.wait_ge(mv_ready, b)
                for t in range(KT):
                    last = nc.vector.bn_stats(stats[:, t, :], x_all[:, b * KT + t, :])
                last.then_inc(stats_ready, 1)
                dve.wait_ge(stats_ready, b + 1)
                for t in range(KT):
                    last = nc.vector.bn_aggr(mv[:, b % 2, t, :], stats[:, t, :])
                last.then_inc(mv_ready, 1)

            def batch_xn(b):
                dve.wait_ge(rstd_ready, b + 1)
                dve.wait_ge(mv_ready, b + 1)
                if b > 0:
                    dve.wait_ge(xt_mm, 2 * b)
                for t in range(KT):
                    last = nc.vector.tensor_scalar(xn[:, t, :], x_all[:, b * KT + t, :], mv[:, b % 2, t, 0:1],
                                                   rstd[:, b % 2, t:t + 1], ALU.subtract, ALU.mult)
                last.then_inc(xn_ready, 1)

            batch_stats(0)
            dve.wait_ge(w_attn_loaded, 16 * N_ATTN_W)
            for w in range(2):
                nc.vector.tensor_copy(wqk[:, w, :].rearrange("p (g e h) -> p g e h", e=D, h=HG),
                                      wqkv[:, w * E:(w + 1) * E].rearrange("p (g h e) -> p g e h", e=D, h=HG)
                                      ).then_inc(perm_ready, 1)
                nc.vector.tensor_copy(brow_qk[:, w, :].rearrange("p (g e h) -> p g e h", e=D, h=HG),
                                      brow[:, w * E:(w + 1) * E].rearrange("p (g h e) -> p g e h", e=D, h=HG)
                                      ).then_inc(perm_ready, 1)
            batch_xn(0)
            dve.wait_ge(setup_mm, 1)
            nc.vector.tensor_copy(bqk[:, :], ps[:, 7, 0:2]).then_inc(setup_copied, 1)
            batch_stats(1)
            batch_xn(1)
            batch_stats(2)

            def residual(b, w):
                dve.wait_ge(part1_ready, 2 * b + w + 1)
                if b > 0:
                    dve.wait_ge(part2_ready, 2 * b + w - 1)
                    dve.wait_ge(part3_ready, 2 * b + w - 1)
                nc.vector.tensor_tensor(qkr[:, w, :], qkf[:, w, :], qkp[:, b % 2, 0, w, :],
                                        ALU.subtract).then_inc(res1_ready, 1)

            dve.wait_ge(vones_ready, 1)
            for b in range(B):
                s = b % 2
                residual(b, 0)
                if b == 0:
                    batch_stats(3)
                residual(b, 1)
                if b + 2 < B:
                    batch_xn(b + 2)
                dve.wait_ge(v_mm, b + 1)
                if b > 1:
                    dve.wait_ge(parts_stored[s], 16 * STORES * (b // 2))
                for t in range(KT):
                    last = nc.vector.tensor_tensor(
                        vst[:, s, :, t, :, 0:D],
                        ps[:, 6 + t // 4, (t % 4) * P:(t % 4 + 1) * P].rearrange("p (g h e) -> p g h e", h=HG, e=D),
                        bv[:, :].rearrange("p (g h e) -> p g h e", h=HG, e=D), ALU.add)
                last.then_inc(v_copied, 1)


            def split_maxima(turn, du, step):
                if step == 0:
                    dve.wait_ge(max_read, turn * TURN_FILLS + fill_of(du * STEPS + STEPS - 1, 3) + 1)
                    ins = nc.vector.tensor_reduce(negm[:, :], mx[:, du % 2, :, :], AX.X, ALU.max, negate=True)
                else:
                    dve.wait_ge(mchain, turn * (4 * CH) + du * CH + step)
                if step == 1:
                    ins = nc.vector.tensor_copy(mparts[:, 0:HG * QT], negm[:, :])
                if step == 2:
                    ins = nc.vector.tensor_tensor(mres[:, :], negm[:, :], mparts[:, 0:HG * QT], ALU.subtract)
                if step == 3:
                    ins = nc.vector.tensor_copy(mparts[:, HG * QT:2 * HG * QT], mres[:, :])
                if step == 4:
                    ins = nc.vector.tensor_tensor(mparts[:, 2 * HG * QT:3 * HG * QT], mres[:, :],
                                                  mparts[:, HG * QT:2 * HG * QT], ALU.subtract)
                ins.then_inc(mchain, 1)

            def copy_m(turn, du, last=False):
                n = fill_of_m(du, last)
                dve.wait_ge(max_scores, turn * TURN_FILLS + n + 1)
                nc.vector.tensor_copy(mrow[:, :], ps[:, ROT[n % 3], :].bitcast(BF16)[0:PARTS * HG * QT, 0:P]
                                      ).then_inc(max_read, 1)

            def maxima(turn, c):
                r, u = c % STEPS, c // STEPS
                for k in range(4):
                    n = fill_of(c, k)
                    dve.wait_ge(max_scores, turn * TURN_FILLS + n + 1)
                    col = (r // 2) * QT + (r % 2) * 2 + k // 2
                    nc.vector.tensor_reduce(mx[:, u % 2, col, k % 2:k % 2 + 1], ps[:, ROT[n % 3], :], AX.X,
                                            ALU.max).then_inc(max_read, 1)
                    if c >= STEPS and 4 * r + k < CH:
                        split_maxima(turn, u - 1, 4 * r + k)
                if r == 1 and c > 1:
                    copy_m(turn, u - 1)

            for c in range(LEAD):
                maxima(0, c)
            dve.wait_ge(v_copied, B)
            nc.vector.memset(ps[:, 6, :], 0.0).then_inc(o_bank_free, 1)
            with dve.Fori(0, TURNS - 1) as turn:
                for s in range(STEP_IT):
                    maxima(turn, s + LEAD)
            for s in range(STEP_IT - LEAD):
                maxima(TURNS - 1, s + LEAD)
            for step in range(CH):
                split_maxima(TURNS - 1, 3, step)
            copy_m(TURNS - 1, 3, True)

            dve.wait_ge(w_out_loaded, 32)
            dve.wait_ge(bf_step, BF_STEPS)
            dve.wait_ge(ffn_mm, 2)
            nc.vector.tensor_copy(wdn[:, :, :].rearrange("p c e -> p (c e)"), ps[:, 7, :]).then_inc(ffn_w_ready, 1)
            nc.vector.tensor_copy(bup[:, :], ps[:, 0, 0:HC]).then_inc(ffn_w_ready, 1)

            def divide(t):
                dve.wait_ge(o_tr, t + 1)
                o = ps[:, 0:2, 0:2 * H * VW].rearrange("p k (t c) -> p k t c", c=VW)
                r = rec[:, :].rearrange("p (k t) -> p k t", k=2)
                nc.vector.reciprocal(r, o[:, :, :, D]).then_inc(rec_ready, 1)
                dve.wait_ge(rec_ready, t + 1)
                nc.vector.tensor_tensor(att.rearrange("p (k t) (h d) -> p k (t h) d", k=2, d=D),
                                        o[:, :, :, 0:D], r.unsqueeze(3).to_broadcast([P, 2, 2 * H, D]),
                                        ALU.mult).then_inc(att_ready, 1)

            def read_y(t, first=False):
                if not first:
                    dve.wait_ge(x1_ready, t)
                dve.wait_ge(y_mm, t + 1)
                nc.vector.tensor_tensor(yb, ps[:, 0, :].rearrange("p (t e) -> p t e", e=E),
                                        bout[:, :].unsqueeze(1).to_broadcast([P, BT, E]), ALU.add
                                        ).then_inc(y_read, 1)

            def read_y2(t, first=False):
                if not first:
                    dve.wait_ge(y2_normed, t)
                dve.wait_ge(y2_mm, t + 1)
                nc.vector.tensor_tensor(y2[:, :, :], ps[:, 5, :].rearrange("p (t e) -> p t e", e=E),
                                        bffn[:, :].unsqueeze(1).to_broadcast([P, BT, E]), ALU.add
                                        ).then_inc(y2_read, 1)

            def pair_stats(k, two, one, div, back=0):
                if one:
                    read_y(k + 2, first=not two)
                if two:
                    dve.wait_ge(x1_ready, k + 2)
                    for tt in range(BT):
                        last = nc.vector.bn_stats(st3[:, 0, tt, :], x_all[:, bass.ds((k + 1) * BT + tt, 1), :]
                                                  .rearrange("p o e -> p (o e)"))
                if one:
                    dve.wait_ge(y_read, k + 3)
                    for tt in range(BT):
                        last = nc.vector.bn_stats(st3[:, 1, tt, :], yb[:, tt, :])
                last.then_inc(st_ready, 1)
                dve.wait_ge(st_ready, k + 3)
                nc.vector.tensor_copy(carrier[:, :], st3[:, 1, 0, 0:1])
                for norm in ((0,) if two else ()) + ((1,) if one else ()):
                    for tt in range(BT):
                        last = nc.vector.bn_aggr(mv3[:, norm, tt, :], st3[:, norm, tt, :])
                last.then_inc(mv_pair, 1)
                if div:
                    divide(k + 3)
                if back:
                    read_y2(k - 1, first=back == 1)

            def norm1(k):
                dve.wait_ge(rs_pair, k + 3)
                for tt in range(BT):
                    last = nc.vector.tensor_scalar(yb[:, tt, :], yb[:, tt, :], mv3[:, 1, tt, 0:1],
                                                   rs3[:, 1, tt:tt + 1], ALU.subtract, ALU.mult)
                last.then_inc(y_normed, 1)

            def out_stats(t):
                dve.wait_ge(y2_read, t + 1)
                for tt in range(BT):
                    last = nc.vector.bn_stats(st3[:, 2, tt, :], y2[:, tt, :])
                last.then_inc(st_out, 1)
                dve.wait_ge(st_out, t + 1)
                nc.vector.tensor_copy(carrier[:, :], st3[:, 2, 0, 0:1])
                for tt in range(BT):
                    last = nc.vector.bn_aggr(mv3[:, 2, tt, :], st3[:, 2, tt, :])
                last.then_inc(mv_out, 1)

            def copy_att(t):
                dve.wait_ge(att_tr, t + 1)
                nc.vector.tensor_copy(att_t, ps[:, 7, :]).then_inc(att_t_ready, 1)

            divide(0)
            copy_att(0)
            pair_stats(-2, False, True, True)
            copy_att(1)
            norm1(-2)
            pair_stats(-1, True, True, True)
            copy_att(2)
            for tt in range(BT):
                if tt == 0:
                    dve.wait_ge(rs_pair, 2)
                last = nc.vector.tensor_scalar(x1n[:, tt, :], x_all[:, tt, :], mv3[:, 0, tt, 0:1],
                                               rs3[:, 0, tt:tt + 1], ALU.subtract, ALU.mult)
            last.then_inc(x1n_ready, 1)
            norm1(-1)
            dve.wait_ge(x1_tr, 1)
            nc.vector.tensor_copy(x1t[:, :], ps[:, 7, :]).then_inc(x1t_ready, 1)

            def turn_dve(k, div, one, two, back):
                if two:
                    pair_stats(k, two, one, div, back)
                elif back:
                    read_y2(k - 1)
                if back:
                    out_stats(k - 1)
                if one:
                    norm1(k)

            turn_dve(0, True, True, True, 0)
            turn_dve(1, True, True, True, 1)
            with dve.Fori(2, BLOCKS - 3) as k:
                turn_dve(k, True, True, True, 2)
            for k in range(BLOCKS - 3, BLOCKS + 1):
                turn_dve(k, False, k + 2 < BLOCKS, k + 1 < BLOCKS, 2)
            dve.wait_ge(rs_out, BLOCKS)
            for tt in range(BT):
                last = nc.vector.tensor_scalar(y2[:, tt, :], y2[:, tt, :], mv3[:, 2, tt, 0:1],
                                               rs3[:, 2, tt:tt + 1], ALU.subtract, ALU.mult)
            last.then_inc(y2_normed, 1)
            dve.wait_ge(y2_normed, BLOCKS)
            nc.vector.tensor_tensor(x_all[:, (BLOCKS - 1) * BT:, :], x_all[:, (BLOCKS - 1) * BT:, :], y2[:, :, :],
                                    ALU.add).then_inc(res_ready, 1)

        @block.tensor
        def _(pe):
            pe.wait_ge(perm_ready, 4)
            pe.wait_ge(consts_ready, 8)
            for w in range(2):
                last = nc.tensor.matmul(ps[:, 7, w:w + 1], brow_qk[0:1, w, :], one[:, :], start=True, stop=True)
            last.then_inc(setup_mm, 1)

            def transpose_xn(b):
                pe.wait_ge(xn_ready, b + 1)
                for t in range(KT):
                    last = nc.tensor.transpose(ps[:, t // 4, (t % 4) * P:(t % 4 + 1) * P], xn[:, t, :], ident[:, :])
                    if t % 4 == 3:
                        last.then_inc(xt_mm, 1)

            transpose_xn(0)
            for b in range(B):
                pe.wait_ge(xt_ready, 2 * b + 2)
                for w in range(2):
                    if b > 0:
                        pe.wait_ge(qkf_ready, 2 * b + w - 1)
                    for k in range(2):
                        last = nc.tensor.matmul(ps[:, 2 + 2 * w + k, :], wqk[:, w, :],
                                                xt[:, b % 2, k * 512:(k + 1) * 512], start=True, stop=True)
                    last.then_inc(qk_mm, 1)
                if b + 1 < B:
                    transpose_xn(b + 1)
                if b == 0:
                    pe.wait_ge(setup_copied, 1)
                else:
                    pe.wait_ge(v_copied, b)
                for t in range(KT):
                    last = nc.tensor.matmul(ps[:, 6 + t // 4, (t % 4) * P:(t % 4 + 1) * P],
                                            xt[:, b % 2, t * P:(t + 1) * P], wqkv[:, 2 * E:3 * E],
                                            start=True, stop=True)
                last.then_inc(v_mm, 1)
            pe.wait_ge(w_ffn_loaded, 16 * N_FFN_W)
            for c in range(HC):
                last = nc.tensor.transpose(ps[:, 0, c * P:(c + 1) * P], wcon[:, c, :], ident[:, :])
            last.then_inc(setup_mm, 1)
            pe.wait_ge(setup_copied, 2)
            pe.wait_ge(qkf_ready, 2 * B)
            pe.wait_ge(v_copied, B)

            def transpose_m(turn, du, last=False):
                n = fill_of_m(du, last)
                pe.wait_ge(mchain, turn * (4 * CH) + (du + 1) * CH)
                pe.wait_ge(max_read, turn * TURN_FILLS + n - 2)
                nc.tensor.transpose(ps[:, ROT[n % 3], :].bitcast(BF16)[0:MW, 0:P], mparts[:, :],
                                    ident_bf[:, :]).then_inc(max_scores, 1)

            def max_fill(turn, c, k):
                r, slot, j, half = c % STEPS, (c // (2 * STEPS)) % 2, k // 2, k % 2
                if c % (2 * STEPS) == 0 and k == 0:
                    pe.wait_ge(kq_loaded[slot], (turn + c // STEP_IT + 1) * KQ)
                h, qt, qhalf = r // 2, (r % 2) * 2 + j, (c // STEPS) % 2
                n = fill_of(c, k)
                if n > 2:
                    pe.wait_ge(max_read, turn * TURN_FILLS + n - 2)
                nc.tensor.matmul(ps[:, ROT[n % 3], :], qx[0:PROD, slot, qhalf, h, qt * P:(qt + 1) * P],
                                 kx[0:PROD, slot, h, half * 512:(half + 1) * 512],
                                 start=True, stop=True).then_inc(max_scores, 1)
                if r == 1 and k == 3 and c > 1:
                    transpose_m(turn, c // STEPS - 1)

            def score_pair(turn, s, j):
                slot, half, kt = s // (2 * STEPS), s // STEPS % 2, s % STEPS
                if kt == 0 and j == 0:
                    pe.wait_ge(m_rows_loaded, (turn * 4 + s // STEPS + 1) * MROW)
                if s > 0:
                    pe.wait_ge(exp_done, turn * (2 * STEP_IT) + 2 * s + j - 1)
                for h in range(2):
                    last = nc.tensor.matmul(ps[:, 2 + 2 * j + h, :], kx[0:ROWS, slot, 2 * j + h, kt * P:(kt + 1) * P],
                                            qx[0:ROWS, slot, half, 2 * j + h, :],
                                            start=True, stop=True)
                last.then_inc(exp_scores, 1)

            def weigh_v(turn, s):
                slot, kt = s // (2 * STEPS), s % STEPS
                pe.wait_ge(exp_done, turn * (2 * STEP_IT) + 2 * s + 2)
                if s % (2 * STEPS) == 0:
                    pe.wait_ge(v_loaded[slot], (turn + 1) * 16)
                if kt == 0:
                    pe.wait_ge(o_bank_free, turn * 4 + s // STEPS + 1)
                for h in range(HG):
                    last = nc.tensor.matmul(ps[32 * h:32 * h + VW, 6, :], vg[:, slot, kt, h, :],
                                            pr[:, 2 * (s % 2) + h // 2, h % 2, :],
                                            start=(kt == 0), stop=(kt == STEPS - 1))
                last.then_inc(pv_done, 1)

            def turn_pe(turn, last_turn):
                for s in range(STEP_IT):
                    ahead = not last_turn or s + LEAD < STEP_IT
                    end = s == STEP_IT - 1

                    def maxima(k):
                        if ahead:
                            max_fill(turn, s + LEAD, k)

                    score_pair(turn, s, 0)
                    maxima(0)
                    score_pair(turn, s, 1)
                    if not end:
                        maxima(1)
                        if s > 0:
                            weigh_v(turn, s - 1)
                        maxima(2)
                        maxima(3)
                    else:
                        weigh_v(turn, s - 1)
                        maxima(1)
                        maxima(2)
                        maxima(3)
                        if last_turn:
                            project_out(2)
                            transpose_x1(0)
                        weigh_v(turn, s)
                    if last_turn and s + LEAD == STEP_IT:
                        transpose_m(turn, 3, True)
                    if last_turn:
                        beside_attention(s - (STEP_IT - LEAD + 1))

            def feedforward_weights():
                pe.wait_ge(w_out_loaded, 32)
                pe.wait_ge(bf_step, BF_STEPS)
                pe.wait_ge(max_read, TURN_FILLS * TURNS)
                for c in range(HC):
                    last = nc.tensor.transpose(ps[:, 7, c * P:(c + 1) * P], dn_y[:, 0, c * P:(c + 1) * P],
                                               ident[:, :])
                last.then_inc(ffn_mm, 1)
                for c in range(HC):
                    last = nc.tensor.matmul(ps[:, 0, c:c + 1], row_y[0:1, 1, c * P:(c + 1) * P], one[:, :],
                                            start=True, stop=True)
                last.then_inc(ffn_mm, 1)

            def untranspose(t, slot, use, first=False):
                pe.wait_ge(o_in_loaded[slot], (use + 1) * 32)
                if first:
                    pe.wait_ge(ffn_w_ready, 2)
                else:
                    pe.wait_ge(y_read, t)
                rows = 2 * HG * VW
                for tt in range(BT):
                    for j in range(2):
                        c = (tt % 2) * 2 * rows + j * rows
                        last = nc.tensor.transpose(ps[:, tt // 2, c:c + rows], o_in[:, slot, j, tt * P:(tt + 1) * P],
                                                   ident[0:rows, 0:rows])
                last.then_inc(o_tr, 1)

            def transpose_att(t):
                pe.wait_ge(att_ready, t + 1)
                for tt in range(BT):
                    last = nc.tensor.transpose(ps[:, 7, tt * P:(tt + 1) * P], att[:, tt, :], ident[:, :])
                last.then_inc(att_tr, 1)

            def project_out(t):
                pe.wait_ge(att_t_ready, t + 1)
                for tt in range(BT):
                    last = nc.tensor.matmul(ps[:, 0, tt * P:(tt + 1) * P], att_t[:, tt * P:(tt + 1) * P], wout[:, :],
                                            start=True, stop=True)
                last.then_inc(y_mm, 1)

            def transpose_x1(t):
                pe.wait_ge(x1n_ready, t + 1)
                for tt in range(BT):
                    last = nc.tensor.transpose(ps[:, 7, tt * P:(tt + 1) * P], x1n[:, tt, :], ident[:, :])
                last.then_inc(x1_tr, 1)

            def beside_attention(n):
                if n == 0:
                    feedforward_weights()
                elif 1 <= n <= 9 and n % 3 == 1:
                    t = n // 3
                    untranspose(t, t % 2, t // 2, first=t == 0)
                elif 1 <= n <= 9 and n % 3 == 2:
                    transpose_att(n // 3)
                elif 1 <= n < 9:
                    project_out(n // 3 - 1)

            for c in range(LEAD):
                for k in range(4):
                    max_fill(0, c, k)
            with pe.Fori(0, TURNS - 1) as turn:
                turn_pe(turn, False)
            turn_pe(TURNS - 1, True)

            pe.wait_ge(exp_done, 2 * STEP_IT * TURNS)

            def hidden(t, i, first=False):
                c, start, n, bank = PIECES[i]
                if first:
                    pe.wait_ge(o_bank_free, UNITS + 1)
                if i == 0:
                    pe.wait_ge(x1t_ready, t + 1)
                if i == 4:
                    pe.wait_ge(gelu_done, t * len(PIECES) + 1)
                nc.tensor.matmul(ps[:, bank, start:start + n], up_y[:, 0, c * P:(c + 1) * P],
                                 x1t[:, start:start + n],
                                 start=True, stop=True).then_inc(h_mm, 1)

            def contract(t, tt):
                for c in range(HC):
                    last = nc.tensor.matmul(ps[:, 5, tt * P:(tt + 1) * P], gt[:, c, tt * P:(tt + 1) * P],
                                            wdn[:, c, :], start=(c == 0), stop=(c == HC - 1))
                return last

            def turn_pe_ffn(k, front, slot, use, first=False, last=False):
                hidden(k, 0)
                hidden(k, 1)
                if front:
                    untranspose(k + 3, slot, use)
                hidden(k, 2)
                hidden(k, 3, first)
                hidden(k, 4)
                if front:
                    transpose_att(k + 3)
                pe.wait_ge(gelu_done, k * len(PIECES) + len(PIECES) - 1)
                if not first:
                    pe.wait_ge(y2_read, k)
                contract(k, 0)
                contract(k, 1)
                if front:
                    project_out(k + 3)
                pe.wait_ge(gelu_done, (k + 1) * len(PIECES))
                contract(k, 2)
                if not last:
                    transpose_x1(k + 1)
                contract(k, 3).then_inc(y2_mm, 1)

            turn_pe_ffn(0, True, 1, 1, first=True)
            with pe.Fori(0, (BLOCKS - 4) // 2) as i:
                turn_pe_ffn(i * 2 + 1, True, 0, i + 2)
                turn_pe_ffn(i * 2 + 2, True, 1, i + 2)
            for k in range(BLOCKS - 3, BLOCKS):
                turn_pe_ffn(k, False, 0, 0, last=k == BLOCKS - 1)

    return nc


NAMES = ["L0_attn_x", "L0_attn_W_qkv", "L0_attn_b_qkv", "L0_attn_W_out", "L0_attn_b_out", "L0_ffn_W_exp",
         "L0_ffn_b_exp", "L0_ffn_up_weights", "L0_ffn_up_bias", "L0_ffn_down_weights", "L0_ffn_W_con",
         "L0_ffn_b_con", "L0_ffn_down_bias"]


def kernel(**inputs):
    import concourse.bacc as bacc
    from concourse.bass_utils import run_bass_kernel_spmd

    nc = bacc.Bacc("TRN2", target_bir_lowering=False, num_devices=1)
    arrays, args = {}, []
    for name in NAMES:
        a = np.ascontiguousarray(inputs[name])
        arrays[name] = a
        args.append(nc.dram_tensor(name, a.shape, mybir.dt.from_np(a.dtype), kind="ExternalInput").ap())
    out = nc.dram_tensor("out", (B, N, E), FP32, kind="ExternalOutput").ap()
    attention_ffn_kernel(nc, *args, out)
    got = run_bass_kernel_spmd(nc, [arrays], core_ids=[0])
    return got.results[0]["out"]
```
